# Optimizing a Trainium2 kernel written in Bass

```python
import numpy as np
import jax
import jax.numpy as jnp

def _softmax(x, axis=-1):
    return jax.nn.softmax(x, axis=axis)
def _gelu(x):
    return jax.nn.gelu(x, approximate=True)
def _silu(x):
    return jax.nn.silu(x)
def _sigmoid(x):
    return jax.nn.sigmoid(x)
def _layernorm(x, axis=-1, eps=1e-5):
    m = jnp.mean(x, axis=axis, keepdims=True)
    v = jnp.var(x, axis=axis, keepdims=True)
    return (x - m) / jnp.sqrt(v + eps)
def _scatter_add(tgt, idx, src, axis=0):
    return tgt.at[idx].add(src)
def _segment_sum(src, seg, n):
    return jax.ops.segment_sum(src, seg, n)

kernel_name = 'mk_early_fusion_d1_tok_img256_7d6ab7'

def setup_inputs(seed: int = 0):
    np.random.seed(seed)
    _w = jnp.asarray
    def _rec_inputs():
        import jax
        import jax.numpy as jnp
        _rk = jax.random.key(seed)
        x = (7.22013e-05 + 1.00017 * jax.random.normal(jax.random.fold_in(_rk, 1), (4, 256, 64, 64), jnp.float32))
        txt = (-0.0348604 + 0.77908 * jax.random.normal(jax.random.fold_in(_rk, 2), (4, 512, 256), jnp.float32))
        return x, txt
    x, txt = _rec_inputs()
    def _L0_tok_setup():
        import jax, jax.numpy as jnp
        import numpy as np
        B, C, H, W = (8, 256, 64, 64)
        NB = 3
        E = 256
        key = jax.random.key(seed)
        ks = jax.random.split(key, 6)
        x = jax.random.normal(ks[0], (B, C, H, W), dtype=jnp.float32)
        bases = jax.random.normal(ks[1], (C, NB), dtype=jnp.float32)
        W_spline = jax.random.normal(ks[2], (E, C * NB), dtype=jnp.float32) * (1.0 / np.sqrt(C * NB))
        b_spline = jax.random.normal(ks[3], (E,), dtype=jnp.float32) * 0.01
        W_base = jax.random.normal(ks[4], (E, C), dtype=jnp.float32) * (1.0 / np.sqrt(C))
        b_base = jax.random.normal(ks[5], (E,), dtype=jnp.float32) * 0.01
        return {'x': x, 'bases': bases, 'W_spline': W_spline, 'b_spline': b_spline, 'W_base': W_base, 'b_base': b_base}
    _L0_tok_all = _L0_tok_setup()
    _L0_tok_in = {k: v for k, v in _L0_tok_all.items() if k in ('bases', 'W_spline', 'b_spline', 'W_base', 'b_base', )}
    del _L0_tok_all

    def _L0_attn_setup():
        import jax, jax.numpy as jnp
        import numpy as np
        DIM = 256
        HEADS = 4
        DIM_HEAD = 32
        NUM_MEM = 4
        HIDDEN = HEADS * DIM_HEAD
        SCALE = DIM_HEAD ** (-0.5)

        def rmsnorm(x, g):
            n = jnp.linalg.norm(x, axis=-1, keepdims=True)
            return x / jnp.maximum(n, 1e-12) * g * x.shape[-1] ** 0.5
        key = jax.random.key(seed)
        ks = jax.random.split(key, 8)
        B, N = (4, 16384)
        return {'x': jax.random.normal(ks[0], (B, N, DIM), jnp.float32), 't': jax.random.normal(ks[1], (B,), jnp.float32), 'w_qkv': jax.random.normal(ks[2], (DIM, 3 * HIDDEN), jnp.float32) * 0.02, 'mem_kv': jax.random.normal(ks[3], (2, HEADS, DIM_HEAD, NUM_MEM), jnp.float32), 'w_out': jax.random.normal(ks[4], (HIDDEN, DIM), jnp.float32) * 0.02, 'b_out': jnp.zeros((DIM,), jnp.float32), 'g_out': jnp.ones((DIM,), jnp.float32), 'g_pre': jnp.ones((DIM,), jnp.float32)}
    _L0_attn_all = _L0_attn_setup()
    _L0_attn_in = {k: v for k, v in _L0_attn_all.items() if k in ('t', 'w_qkv', 'mem_kv', 'w_out', 'b_out', 'g_out', 'g_pre', )}
    del _L0_attn_all

    def _L0_ffn_setup():
        import jax, jax.numpy as jnp
        import numpy as np
        B, T, D, H, L = (16, 4096, 256, 256, 2)

        def _lstm(x, W_ih, W_hh, b_ih, b_hh):
            x_proj = jnp.einsum('btd,gd->btg', x, W_ih) + b_ih + b_hh
            h0 = jnp.zeros((x.shape[0], W_hh.shape[1]), x.dtype)
            c0 = jnp.zeros_like(h0)

            def step(carry, xp):
                h, c = carry
                gates = xp + h @ W_hh.T
                i, f, g, o = jnp.split(gates, 4, axis=-1)
                c = jax.nn.sigmoid(f) * c + jax.nn.sigmoid(i) * jnp.tanh(g)
                h = jax.nn.sigmoid(o) * jnp.tanh(c)
                return ((h, c), h)
            _, hs = jax.lax.scan(step, (h0, c0), jnp.swapaxes(x_proj, 0, 1))
            return jnp.swapaxes(hs, 0, 1)
        key = jax.random.key(seed)
        ks = jax.random.split(key, 9)
        s = 1.0 / np.sqrt(H)
        u = lambda k, shape: jax.random.uniform(k, shape, jnp.float32, -s, s)
        return {'x': jax.random.normal(ks[0], (B, T, D), jnp.float32), 'W_ih': u(ks[1], (4 * H, D)), 'W_hh': u(ks[2], (4 * H, H)), 'b_ih': u(ks[3], (4 * H,)), 'b_hh': u(ks[4], (4 * H,)), 'W_lin': u(ks[5], (L, H)), 'b_lin': u(ks[6], (L,)), 'fw_att': jnp.full((1, H), 0.001, jnp.float32), 'bw_att': jnp.full((1, H), 0.001, jnp.float32)}
    _L0_ffn_all = _L0_ffn_setup()
    _L0_ffn_in = {k: v for k, v in _L0_ffn_all.items() if k in ('W_ih', 'W_hh', 'b_ih', 'b_hh', 'W_lin', 'b_lin', 'fw_att', 'bw_att', )}
    del _L0_ffn_all

    return {
        "x": x,
        "txt": txt,
        "L0_tok_bases": _L0_tok_in["bases"],
        "L0_tok_W_spline": _L0_tok_in["W_spline"],
        "L0_tok_b_spline": _L0_tok_in["b_spline"],
        "L0_tok_W_base": _L0_tok_in["W_base"],
        "L0_tok_b_base": _L0_tok_in["b_base"],
        "L0_attn_t": _L0_attn_in["t"],
        "L0_attn_w_qkv": _L0_attn_in["w_qkv"],
        "L0_attn_mem_kv": _L0_attn_in["mem_kv"],
        "L0_attn_w_out": _L0_attn_in["w_out"],
        "L0_attn_b_out": _L0_attn_in["b_out"],
        "L0_attn_g_out": _L0_attn_in["g_out"],
        "L0_attn_g_pre": _L0_attn_in["g_pre"],
        "L0_ffn_W_ih": _L0_ffn_in["W_ih"],
        "L0_ffn_W_hh": _L0_ffn_in["W_hh"],
        "L0_ffn_b_ih": _L0_ffn_in["b_ih"],
        "L0_ffn_b_hh": _L0_ffn_in["b_hh"],
        "L0_ffn_W_lin": _L0_ffn_in["W_lin"],
        "L0_ffn_b_lin": _L0_ffn_in["b_lin"],
        "L0_ffn_fw_att": _L0_ffn_in["fw_att"],
        "L0_ffn_bw_att": _L0_ffn_in["bw_att"],
    }

def reference(x, txt, L0_tok_bases, L0_tok_W_spline, L0_tok_b_spline, L0_tok_W_base, L0_tok_b_base, L0_attn_t, L0_attn_w_qkv, L0_attn_mem_kv, L0_attn_w_out, L0_attn_b_out, L0_attn_g_out, L0_attn_g_pre, L0_ffn_W_ih, L0_ffn_W_hh, L0_ffn_b_ih, L0_ffn_b_hh, L0_ffn_W_lin, L0_ffn_b_lin, L0_ffn_fw_att, L0_ffn_bw_att):
    import jax
    import jax.numpy as jnp
    def _L0_tok_ref(x, bases, W_spline, b_spline, W_base, b_base):
        import jax, jax.numpy as jnp
        import numpy as np
        B, C, H, W = (8, 256, 64, 64)
        NB = 3
        E = 256
        b, c, h, w = x.shape
        x_flat = jnp.transpose(x.reshape(b, c, h * w), (0, 2, 1))
        base_out = jnp.einsum('blc,ec->ble', jax.nn.silu(x_flat), W_base) + b_base
        spline = jax.nn.sigmoid(x_flat[..., None] * bases[None, None, :, :])
        spline_flat = spline.reshape(b, h * w, c * bases.shape[1])
        spline_proj = jnp.einsum('blk,ek->ble', spline_flat, W_spline) + b_spline
        return base_out + spline_proj

    def _L0_attn_ref(x, t, w_qkv, mem_kv, w_out, b_out, g_out, g_pre):
        import jax, jax.numpy as jnp
        import numpy as np
        DIM = 256
        HEADS = 4
        DIM_HEAD = 32
        NUM_MEM = 4
        HIDDEN = HEADS * DIM_HEAD
        SCALE = DIM_HEAD ** (-0.5)

        def rmsnorm(x, g):
            n = jnp.linalg.norm(x, axis=-1, keepdims=True)
            return x / jnp.maximum(n, 1e-12) * g * x.shape[-1] ** 0.5
        b, n, c = x.shape
        xn = rmsnorm(x, g_pre)
        qkv = xn @ w_qkv
        q, k, v = jnp.split(qkv, 3, axis=-1)

        def to_heads(z):
            return z.reshape(b, n, HEADS, DIM_HEAD).transpose(0, 2, 3, 1)
        q, k, v = map(to_heads, (q, k, v))
        mk = jnp.broadcast_to(mem_kv[0], (b, HEADS, DIM_HEAD, NUM_MEM))
        mv = jnp.broadcast_to(mem_kv[1], (b, HEADS, DIM_HEAD, NUM_MEM))
        k = jnp.concatenate([mk, k], axis=-1)
        v = jnp.concatenate([mv, v], axis=-1)
        q = jax.nn.softmax(q, axis=-2) * SCALE
        k = jax.nn.softmax(k, axis=-1)
        context = jnp.einsum('bhdn,bhen->bhde', k, v)
        out = jnp.einsum('bhde,bhdn->bhen', context, q)
        out = out.transpose(0, 3, 1, 2).reshape(b, n, HIDDEN)
        out = rmsnorm(out @ w_out + b_out, g_out)
        return out + x

    def _L0_ffn_ref(x, W_ih, W_hh, b_ih, b_hh, W_lin, b_lin, fw_att, bw_att):
        import jax, jax.numpy as jnp
        import numpy as np
        B, T, D, H, L = (16, 4096, 256, 256, 2)

        def _lstm(x, W_ih, W_hh, b_ih, b_hh):
            x_proj = jnp.einsum('btd,gd->btg', x, W_ih) + b_ih + b_hh
            h0 = jnp.zeros((x.shape[0], W_hh.shape[1]), x.dtype)
            c0 = jnp.zeros_like(h0)

            def step(carry, xp):
                h, c = carry
                gates = xp + h @ W_hh.T
                i, f, g, o = jnp.split(gates, 4, axis=-1)
                c = jax.nn.sigmoid(f) * c + jax.nn.sigmoid(i) * jnp.tanh(g)
                h = jax.nn.sigmoid(o) * jnp.tanh(c)
                return ((h, c), h)
            _, hs = jax.lax.scan(step, (h0, c0), jnp.swapaxes(x_proj, 0, 1))
            return jnp.swapaxes(hs, 0, 1)
        lstm_out = _lstm(x, W_ih, W_hh, b_ih, b_hh)
        logits = jnp.einsum('bth,lh->btl', lstm_out, W_lin) + b_lin
        g = jax.lax.stop_gradient(jnp.argmax(logits, axis=-1).astype(lstm_out.dtype))[..., None]
        w = g * lstm_out
        inc = jnp.cumsum(w, axis=1)
        prefix = inc - w
        suffix = inc[:, -1:, :] - inc
        return 2.0 * lstm_out + prefix * fw_att + suffix * bw_att

    h = _L0_tok_ref(x, L0_tok_bases, L0_tok_W_spline, L0_tok_b_spline, L0_tok_W_base, L0_tok_b_base)
    h = jnp.concatenate([h, txt], axis=1)
    h = h + _L0_attn_ref(_layernorm(h, axis=-1), L0_attn_t, L0_attn_w_qkv, L0_attn_mem_kv, L0_attn_w_out, L0_attn_b_out, L0_attn_g_out, L0_attn_g_pre)
    h = h + _L0_ffn_ref(_layernorm(h, axis=-1), L0_ffn_W_ih, L0_ffn_W_hh, L0_ffn_b_ih, L0_ffn_b_hh, L0_ffn_W_lin, L0_ffn_b_lin, L0_ffn_fw_att, L0_ffn_bw_att)
    return h


_drawn_inputs = setup_inputs


def setup_inputs(seed=0):
    import zlib

    import numpy as np

    out = dict(_drawn_inputs(seed))
    spreads = {'L0_attn_b_out': (0.0, 0.1),
     'L0_attn_g_out': (1.0, 0.2),
     'L0_attn_g_pre': (1.0, 0.6),
     'L0_ffn_fw_att': (0.0010000000474974513, 0.6),
     'L0_ffn_bw_att': (0.0010000000474974513, 0.6)}
    factors = {'L0_tok_b_spline': 5.556,
     'L0_tok_b_base': 4.983,
     'L0_attn_mem_kv': 8.0,
     'L0_ffn_b_ih': 3.76,
     'L0_ffn_b_hh': 3.933,
     'L0_ffn_b_lin': 8.0}
    for name, (base, spread) in spreads.items():
        noise = np.random.default_rng([zlib.crc32(name.encode()), seed]).standard_normal(out[name].shape)
        drawn = base * np.exp(spread * noise) if base else spread * noise
        out[name] = jnp.asarray(drawn.astype(out[name].dtype))
    for name, factor in factors.items():
        out[name] = (out[name] * factor).astype(out[name].dtype)
    return out
```

```python
import concourse.bass as bass
from concourse import mybir
from contextlib import ExitStack

F32 = mybir.dt.float32
F16 = mybir.dt.float16
ALU = mybir.AluOpType
ACT = mybir.ActivationFunctionType
AX = mybir.AxisListType

P = 128
E = 256
HALVES = E // P
HEADS, DH, MEM = 4, 32, 4
NB = 3
CH = 256
TPC = CH // P
U = 32
LN_EPS = 1e-5
NORM_MIN = 1e-12
ROOT_E = float(E) ** 0.5

W_SCALE = 2.0 ** 9
H_SCALE = 2.0 ** 10
GATE_SCALE = W_SCALE * H_SCALE


def holder(held):
    def hold(engine, semaphore, value):
        engine.wait_ge(semaphore, value)
        engine.sem_inc(held, 1)
    return hold


def token_phases(nc, ctx_outer, xr, ident, ones, args):
    (x, txt, bases, w_spline, b_spline, w_base, b_base, w_qkv, mem_k, mem_v, w_out, b_out, g_out,
     g_pre, s_dram, h_dram) = args
    B = x.shape[0]
    n_img = x.shape[2]
    n_txt = txt.shape[1]
    CI = n_img // CH
    CT = n_txt // CH
    C = CI + CT
    BPC = CH // U
    assert CI % 2 == 0 and CT % 2 == 0

    with ExitStack() as ctx:
        def sb(name, shape, dt=F32):
            return ctx.enter_context(nc.sbuf_tensor(name, shape, dt))

        def pb(name):
            return ctx.enter_context(nc.psum_tensor(name, [P, 512], F32))

        def sem(name):
            return ctx.enter_context(nc.semaphore(name))

        wsp = sb("wsp", [P, NB, HALVES, E])
        wba = sb("wba", [P, HALVES, E])
        wqkv = sb("wqkv", [P, HALVES, 3 * P])
        wo = sb("wo", [P, E])
        hbase = sb("hbase", [P, HALVES, NB])
        gpre = sb("gpre", [P, HALVES])
        bias_rows = sb("bias_rows", [1, 2, E])
        tok_bias = sb("tok_bias", [P, E])
        bo = sb("bo", [P, E])
        go = sb("go", [P, E])
        mk = sb("mk", [P, MEM])
        mv = sb("mv", [MEM, P])
        head_mask = sb("head_mask", [P, P])
        expo = sb("expo", [P, 2, TPC])
        eps2 = sb("eps2", [P, 2, TPC])
        mem_max = sb("mem_max", [P, 1])
        mem_neg = sb("mem_neg", [P, 1])
        mem_e = sb("mem_e", [P, MEM])
        mem_eT = sb("mem_eT", [MEM, P])
        mem_z = sb("mem_z", [P, 1])
        mem_ctx = sb("mem_ctx", [P, P])
        kmax = sb("kmax", [P, 1])
        knew = sb("knew", [P, 1])
        kchunk = sb("kchunk", [P, 1])
        kneg = sb("kneg", [P, 1])
        kcorr = sb("kcorr", [P, 1])
        zsum = sb("zsum", [P, 1])
        zchunk = sb("zchunk", [P, 1])
        zinv = sb("zinv", [P, 1])
        cacc = sb("cacc", [P, P])
        cnorm = sb("cnorm", [P, P])
        cT = sb("cT", [P, P])
        cw = sb("cw", [P, E])
        xc = [sb(f"xc{i}", [P, HALVES, CH]) for i in range(2)]
        spl = sb("spl", [P, NB, HALVES, CH])
        slu = sb("slu", [P, HALVES, CH])
        ht = sb("ht", [P, TPC, E])
        un = sb("un", [P, TPC, E])
        unT = sb("unT", [P, HALVES, CH])
        st = sb("st", [P, TPC, E])
        vt = sb("vt", [P, TPC, P])
        ek = sb("ek", [P, CH])
        ekT = sb("ekT", [P, TPC, P])
        qt = sb("qt", [P, TPC, P])
        qTt = sb("qTt", [P, CH])
        yt = sb("yt", [P, TPC, E])
        stats = sb("stats", [P, TPC, 6])
        mvar = sb("mvar", [P, TPC, 2])
        vroot = sb("vroot", [P, 2, TPC])
        proot = sb("proot", [P, 2, TPC])
        nrm = sb("nrm", [P, TPC])
        rnrm = sb("rnrm", [P, TPC])
        scl = sb("scl", [P, TPC])
        sone = sb("sone", [P, TPC])
        smean = sb("smean", [P, TPC])
        qmax = sb("qmax", [P, TPC * HEADS])
        qsum = sb("qsum", [P, TPC * HEADS])
        sumsq = sb("sumsq", [P, TPC])

        p_tok, p_uT, p_k, p_q, p_v, p_e, p_c, p_qT = [pb(n) for n in
                                                   ("p_tok", "p_uT", "p_k", "p_q", "p_v", "p_e", "p_c", "p_qT")]

        hold = holder(sem("held"))
        weights_in = sem("weights_in")
        consts = sem("consts")
        prep = sem("prep")
        bias_psum = sem("bias_psum")
        mem_exp = sem("mem_exp")
        mem_tr = sem("mem_tr")
        mem_trs = sem("mem_trs")
        mem_c = sem("mem_c")
        setup_done = sem("setup_done")
        x_in = [sem("x_in0"), sem("x_in1")]
        txt_in = sem("txt_in")
        tanh_ready = sem("tanh_ready")
        silu_ready = sem("silu_ready")
        tok_psum = sem("tok_psum")
        h_ready = sem("h_ready")
        stat_a = sem("stat_a")
        stat_b = sem("stat_b")
        roots_in = sem("roots_in")
        roots = sem("roots")
        small = sem("small")
        un_ready = sem("un_ready")
        s_ready = sem("s_ready")
        s_stored = sem("s_stored")
        uT_psum = sem("uT_psum")
        uT_ready = sem("uT_ready")
        k_psum = sem("k_psum")
        q_psum = sem("q_psum")
        v_psum = sem("v_psum")
        kstep = sem("kstep")
        kneg_ready = sem("kneg_ready")
        ek_ready = sem("ek_ready")
        e_psum = sem("e_psum")
        eT_ready = sem("eT_ready")
        v_ready = sem("v_ready")
        qstep = sem("qstep")
        qs_ready = sem("qs_ready")
        q_exp = sem("q_exp")
        qn_ready = sem("qn_ready")
        qT_psum = sem("qT_psum")
        qT_ready = sem("qT_ready")
        c_psum = sem("c_psum")
        c_done = sem("c_done")
        state0 = sem("state0")
        cn_ready = sem("cn_ready")
        cT_psum = sem("cT_psum")
        cT_ready = sem("cT_ready")
        cw_psum = sem("cw_psum")
        cw_ready = sem("cw_ready")
        s_in = sem("s_in")
        qT_back = sem("qT_back")
        y_psum = sem("y_psum")
        y_ready = sem("y_ready")
        sq_ready = sem("sq_ready")
        ynorm = sem("ynorm")
        ysm = sem("ysm")
        yg_ready = sem("yg_ready")
        h1_ready = sem("h1_ready")
        h1_stored = sem("h1_stored")
        b_un = sem("b_un")
        b_uT = sem("b_uT")
        xr_ready = sem("xr_ready")

        def slots(c, b, half):
            v = xr[:, bass.ds(c * BPC + 1, BPC), half, bass.ds(b, 1), :]
            return v.rearrange("p k a s -> p k (a s)")

        def by_batch(e, image, text, out_):
            with e.Fori(0, B) as b:
                with e.Fori(0, CI // 2) as cp:
                    for par in range(2):
                        image(b, cp, par)
                with e.Fori(0, CT // 2) as cp:
                    for par in range(2):
                        text(b, cp, par)
                out_(b)

        block = ctx.enter_context(nc.Block())

        @block.sync
        def _(sp):
            for dst, src in ((wsp, w_spline), (wba, w_base), (wqkv, w_qkv), (wo, w_out), (hbase, bases),
                             (gpre, g_pre), (mk, mem_k), (mv, mem_v)):
                sp.dma_start(dst[:], src).then_inc(weights_in, 16)
            sp.dma_start(bias_rows[0:1, 0, :], b_spline).then_inc(weights_in, 16)
            sp.dma_start(bias_rows[0:1, 1, :], b_base).then_inc(weights_in, 16)
            sp.dma_start(bo[:], b_out.broadcast_to([P, E])).then_inc(weights_in, 16)
            sp.dma_start(go[:], g_out.broadcast_to([P, E])).then_inc(weights_in, 16)
            sp.wait_ge(consts, 1)
            for b in range(B):
                sp.dma_start(h_dram[b, 0:U, :], st[0:U, 0, :]).then_inc(h1_stored, 16)
            sp.wait_ge(h1_stored, 16 * B)

            def store_s(b, c, n):
                hold(sp, s_ready, n * TPC + TPC)
                sp.dma_start(s_dram[bass.ds(b, 1), bass.ds(c * CH, CH), :].rearrange("a (t p) d -> p (a t) d", p=P),
                             st[:]).then_inc(s_stored, 16)

            def image(b, cp, par):
                xi = sp.snap(b * CI + cp * 2 + par)
                hold(sp, silu_ready, xi + 1)
                sp.dma_start(xc[par][:], x[bass.ds(b, 1), :, bass.ds((cp * 2 + par) * CH, CH)]
                             .rearrange("a (h p) n -> p (a h) n", p=P)).then_inc(x_in[par], 16)
                store_s(b, cp * 2 + par, sp.snap(b * C + cp * 2 + par))

            def text(b, cp, par):
                c = cp * 2 + par
                n = sp.snap(b * C + CI + c)
                hold(sp, un_ready, n)
                hold(sp, s_ready, n * TPC)
                sp.dma_start(ht[:], txt[bass.ds(b, 1), bass.ds(c * CH, CH), :]
                             .rearrange("a (t p) d -> p (a t) d", p=P)).then_inc(txt_in, 16)
                store_s(b, sp.snap(c + CI), n)

            def out_(b):
                hold(sp, s_stored, b * (16 * C) + 16 * C)
                with sp.Fori(0, C) as c:
                    n = sp.snap(b * C + c)
                    hold(sp, h1_ready, n)
                    sp.dma_start(st[:], s_dram[bass.ds(b, 1), bass.ds(c * CH, CH), :]
                                 .rearrange("a (t p) d -> p (a t) d", p=P)).then_inc(s_in, 16)
                    hold(sp, h1_ready, n + 1)
                    sp.dma_start(h_dram[bass.ds(b, 1), bass.ds(c * CH + U, CH), :]
                                 .rearrange("a (t p) d -> p (a t) d", p=P), ht[:]).then_inc(h1_stored, 16)
                hold(sp, h1_stored, b * (16 * C) + 16 * C + 16 * B)

            by_batch(sp, image, text, out_)

        @block.gpsimd
        def _(pool):
            pool.memset(st[:], 0.0).then_inc(consts, 1)
            pool.memset(ident[:], 0.0).then_inc(consts, 1)
            pool.memset(ones[:], 1.0).then_inc(consts, 1)
            pool.memset(head_mask[:], 0.0).then_inc(consts, 1)
            pool.memset(xr[:, xr.shape[1] - 1, :, :, :], 0.0).then_inc(consts, 1)
            pool.memset(expo[:, 0, :], -0.5).then_inc(consts, 1)
            pool.memset(expo[:, 1, :], 0.5).then_inc(consts, 1)
            pool.memset(eps2[:, 0, :], LN_EPS).then_inc(consts, 1)
            pool.memset(eps2[:, 1, :], 0.0).then_inc(consts, 1)
            pool.wait_ge(consts, 9)
            pool.affine_select(out=ident[:], in_=ident[:], compare_op=ALU.not_equal, fill=1.0, base=0,
                               pattern=[[-1, P]], channel_multiplier=1).then_inc(consts, 1)
            for h in range(HEADS):
                pool.wait_ge(consts, 10 + h)
                pool.memset(head_mask[h * DH:(h + 1) * DH, h * DH:(h + 1) * DH], float(DH) ** -0.5)\
                    .then_inc(consts, 1)
            pool.wait_ge(consts, 10 + HEADS)
            pool.wait_ge(h1_stored, 16 * B)

            def roots_of(n):
                pool.wait_ge(roots_in, n + 1)
                pool.tensor_tensor(proot[:], vroot[:], expo[:], ALU.pow).then_inc(roots, 1)

            def residual(b, c):
                n = pool.snap(b * C + c)
                r = pool.snap(b * (2 * C) + c)
                roots_of(r)
                pool.wait_ge(s_stored, n * 16)
                hold(pool, small, n * 6 + 6)
                for t in range(TPC):
                    pool.tensor_scalar(st[:, t, :], ht[:, t, :], sone[:, t:t + 1], smean[:, t:t + 1],
                                       ALU.mult, ALU.add).then_inc(s_ready, 1)

            def image(b, cp, par):
                residual(b, pool.snap(cp * 2 + par))

            def text(b, cp, par):
                residual(b, pool.snap(cp * 2 + par + CI))

            def out_(b):
                with pool.Fori(0, C) as c:
                    n = pool.snap(b * C + c)
                    r = pool.snap(b * (2 * C) + C + c)
                    pool.wait_ge(sq_ready, n + 1)
                    pool.tensor_tensor(nrm[:], sumsq[:], expo[:, 1, :], ALU.pow).then_inc(ynorm, 1)
                    pool.wait_ge(s_in, 16 * n + 16)
                    pool.wait_ge(h1_stored, n * 16 + 16 * B)
                    pool.wait_ge(yg_ready, n + 1)
                    pool.tensor_tensor(ht[:], yt[:], st[:], ALU.add).then_inc(h1_ready, 1)
                    roots_of(r)

            by_batch(pool, image, text, out_)

        @block.scalar
        def _(act):
            act.wait_ge(prep, 6)
            act.activation(mem_e[:], mk[:], ACT.Exp, bias=mem_neg[:, 0:1], accum_out=mem_z[:, 0:1])\
                .then_inc(mem_exp, 1)

            def rest(b, c):
                n = act.snap(b * C + c)
                act.wait_ge(uT_psum, n + 1)
                act.activation(unT[:].rearrange("p h n -> p (h n)"), p_uT[:, 0:HALVES * CH], ACT.Copy)\
                    .then_inc(uT_ready, 1)
                act.wait_ge(v_psum, n + 1)
                act.activation(vt[:].rearrange("p t n -> p (t n)"), p_v[:, 0:CH], ACT.Copy).then_inc(v_ready, 1)
                act.wait_ge(kneg_ready, n + 1)
                act.activation(kcorr[:], kmax[:], ACT.Exp, bias=kneg[:, 0:1])
                act.activation(ek[:], p_k[:, 0:CH], ACT.Exp, bias=kneg[:, 0:1], accum_out=zchunk[:, 0:1])\
                    .then_inc(ek_ready, 1)
                act.wait_ge(qs_ready, n + 1)
                act.activation(qt[:], qt[:], ACT.Exp).then_inc(q_exp, 1)
                act.wait_ge(e_psum, n + 1)
                act.activation(ekT[:].rearrange("p t n -> p (t n)"), p_e[:, 0:CH], ACT.Copy).then_inc(eT_ready, 1)
                hold(act, qT_psum, n + 1)
                act.activation(slots(c, b, 0), p_qT[:, 0:CH].rearrange("p (k s) -> p k s", s=U), ACT.Copy)\
                    .then_inc(qT_ready, 1)

            def image(b, cp, par):
                c = act.snap(cp * 2 + par)
                xi = act.snap(b * CI + c)
                act.wait_ge(tok_psum, xi)
                act.wait_ge(x_in[par], b * (8 * CI) + cp * 16 + 16)
                for j in range(NB):
                    for h in range(HALVES):
                        act.activation(spl[:, j, h, :], xc[par][:, h, :], ACT.Tanh, scale=hbase[:, h, j:j + 1])
                act.activation(slu[:], xc[par][:], ACT.Tanh, scale=0.5).then_inc(tanh_ready, 1)
                rest(b, c)

            def text(b, cp, par):
                rest(b, act.snap(cp * 2 + par + CI))

            def out_(b):
                act.wait_ge(cT_psum, b + 1)
                act.activation(cT[:], p_c[:, 0:P], ACT.Copy).then_inc(cT_ready, 1)
                act.wait_ge(cw_psum, b + 1)
                act.activation(cw[:], p_c[:, P:P + E], ACT.Copy).then_inc(cw_ready, 1)
                with act.Fori(0, C) as c:
                    n = act.snap(b * C + c)
                    act.wait_ge(qT_ready, b * C + C)
                    hold(act, y_psum, n)
                    act.activation(qTt[:].rearrange("p (k s) -> p k s", s=U), slots(c, b, 0), ACT.Copy)\
                        .then_inc(qT_back, 1)
                    act.wait_ge(y_ready, n + 1)
                    for t in range(TPC):
                        ins = act.activation(un[:, t, :], yt[:, t, :], ACT.Square, accum_out=sumsq[:, t:t + 1])
                    ins.then_inc(sq_ready, 1)
                    hold(act, b_uT, n + 1)
                    for h in range(HALVES):
                        ins = act.activation(slots(c, b, h), p_uT[:, h * CH:(h + 1) * CH]
                                             .rearrange("p (k s) -> p k s", s=U), ACT.Copy)
                    ins.then_inc(xr_ready, 1)

            by_batch(act, image, text, out_)

        @block.tensor
        def _(pe):
            pe.wait_ge(consts, 10 + HEADS)
            pe.wait_ge(prep, 5)
            for j in range(NB):
                for h in range(HALVES):
                    pe.matmul(p_tok[:, 0:E], ones[:], wsp[:, j, h, :], start=(j == 0 and h == 0), stop=False)
            for i in range(2):
                mm = pe.matmul(p_tok[:, 0:E], ones[0:1, :], bias_rows[0:1, i, :], start=False, stop=(i == 1))
            mm.then_inc(bias_psum, 1)
            pe.wait_ge(mem_exp, 1)
            pe.transpose(p_c[0:MEM, 0:P], mem_e[:], ident[:]).then_inc(mem_tr, 1)
            pe.wait_ge(mem_trs, 1)
            pe.matmul(p_c[:, P:2 * P], mem_eT[:], mv[:], start=True, stop=True).then_inc(mem_c, 1)
            pe.wait_ge(setup_done, 1)

            def rest(b, c):
                n = pe.snap(b * C + c)
                pe.wait_ge(un_ready, n + 1)
                for h in range(HALVES):
                    for t in range(TPC):
                        mm = pe.transpose(p_uT[:, h * CH + t * P:h * CH + (t + 1) * P],
                                          un[:, t, h * P:(h + 1) * P], ident[:])
                mm.then_inc(uT_psum, 1)
                pe.wait_ge(uT_ready, n + 1)
                for h in range(HALVES):
                    mm = pe.matmul(p_k[:, 0:CH], wqkv[:, h, P:2 * P], unT[:, h, :], start=(h == 0), stop=(h == 1))
                mm.then_inc(k_psum, 1)
                for part, bank, done in ((0, p_q, q_psum), (2, p_v, v_psum)):
                    for t in range(TPC):
                        for h in range(HALVES):
                            mm = pe.matmul(bank[:, t * P:(t + 1) * P], unT[:, h, t * P:(t + 1) * P],
                                           wqkv[:, h, part * P:(part + 1) * P], start=(h == 0), stop=(h == 1))
                    mm.then_inc(done, 1)
                pe.wait_ge(ek_ready, n + 1)
                for t in range(TPC):
                    mm = pe.transpose(p_e[:, t * P:(t + 1) * P], ek[:, t * P:(t + 1) * P], ident[:])
                mm.then_inc(e_psum, 1)
                pe.wait_ge(qn_ready, n + 1)
                for t in range(TPC):
                    mm = pe.transpose(p_qT[:, t * P:(t + 1) * P], qt[:, t, :], ident[:])
                mm.then_inc(qT_psum, 1)
                pe.wait_ge(c_done, n)
                pe.wait_ge(eT_ready, n + 1)
                for t in range(TPC):
                    mm = pe.matmul(p_c[:, 0:P], ekT[:, t, :], vt[:, t, :], start=(t == 0), stop=(t == TPC - 1))
                mm.then_inc(c_psum, 1)

            def image(b, cp, par):
                c = pe.snap(cp * 2 + par)
                xi = pe.snap(b * CI + c)
                pe.wait_ge(h_ready, xi)
                pe.wait_ge(silu_ready, xi + 3)
                for t in range(TPC):
                    tok = slice(t * P, (t + 1) * P)
                    out_ap = p_tok[:, t * E:(t + 1) * E]
                    for j in range(NB):
                        for h in range(HALVES):
                            pe.matmul(out_ap, spl[:, j, h, tok], wsp[:, j, h, :],
                                      start=(j == 0 and h == 0), stop=False)
                    for h in range(HALVES):
                        mm = pe.matmul(out_ap, slu[:, h, tok], wba[:, h, :], start=False, stop=(h == 1))
                mm.then_inc(tok_psum, 1)
                rest(b, c)

            def text(b, cp, par):
                rest(b, pe.snap(cp * 2 + par + CI))

            def out_(b):
                pe.wait_ge(cn_ready, b + 1)
                pe.transpose(p_c[:, 0:P], cnorm[:], ident[:]).then_inc(cT_psum, 1)
                pe.wait_ge(cT_ready, b + 1)
                pe.matmul(p_c[:, P:P + E], cT[:], wo[:], start=True, stop=True).then_inc(cw_psum, 1)
                hold(pe, cw_ready, b + 1)
                with pe.Fori(0, C) as c:
                    n = pe.snap(b * C + c)
                    pe.wait_ge(qT_back, n + 1)
                    for t in range(TPC):
                        mm = pe.matmul(p_tok[:, t * E:(t + 1) * E], qTt[:, t * P:(t + 1) * P], cw[:],
                                       start=True, stop=True)
                    mm.then_inc(y_psum, 1)
                    pe.wait_ge(b_un, n + 1)
                    for h in range(HALVES):
                        for t in range(TPC):
                            mm = pe.transpose(p_uT[:, h * CH + t * P:h * CH + (t + 1) * P],
                                              un[:, t, h * P:(h + 1) * P], ident[:])
                    mm.then_inc(b_uT, 1)

            by_batch(pe, image, text, out_)

        @block.vector
        def _(dve):
            dve.wait_ge(weights_in, 16 * 12)
            dve.tensor_scalar(hbase[:], hbase[:], 0.5, None, ALU.mult).then_inc(prep, 1)
            dve.tensor_scalar(wsp[:].rearrange("p j h e -> p (j h e)"), wsp[:].rearrange("p j h e -> p (j h e)"),
                              0.5, None, ALU.mult).then_inc(prep, 1)
            dve.tensor_scalar(wba[:], wba[:], 0.5, None, ALU.mult).then_inc(prep, 1)
            for h in range(HALVES):
                ins = dve.tensor_scalar(wqkv[:, h, :], wqkv[:, h, :], gpre[:, h:h + 1], None, ALU.mult)
            ins.then_inc(prep, 1)
            dve.tensor_reduce(mem_max[:], mk[:], AX.X, ALU.max).then_inc(prep, 1)
            dve.wait_ge(prep, 5)
            dve.tensor_scalar(mem_neg[:], mem_max[:], -1.0, None, ALU.mult).then_inc(prep, 1)
            dve.tensor_scalar(go[:], go[:], ROOT_E, None, ALU.mult)
            dve.wait_ge(bias_psum, 1)
            dve.tensor_copy(tok_bias[:], p_tok[:, 0:E]).then_inc(prep, 1)
            dve.wait_ge(mem_tr, 1)
            dve.tensor_copy(mem_eT[:], p_c[0:MEM, 0:P]).then_inc(mem_trs, 1)
            dve.wait_ge(mem_c, 1)
            dve.tensor_copy(mem_ctx[:], p_c[:, P:2 * P]).then_inc(setup_done, 1)
            dve.sem_inc(silu_ready, 2)
            dve.wait_ge(setup_done, 1)
            dve.wait_ge(consts, 10 + HEADS)

            def tile_stats(src, k):
                for t in range(TPC):
                    dve.bn_stats(stats[:, t, :], src[:, t, :]).then_inc(stat_a, 1)
                hold(dve, stat_a, k * TPC + TPC)
                for t in range(TPC):
                    dve.bn_aggr(mvar[:, t, :], stats[:, t, :]).then_inc(stat_b, 1)
                dve.wait_ge(stat_b, k * TPC + TPC)
                dve.tensor_tensor(vroot[:], mvar[:, :, 1].unsqueeze(1).broadcast_to([P, 2, TPC]), eps2[:],
                                  ALU.add).then_inc(roots_in, 1)

            def new_state(b):
                dve.wait_ge(h1_stored, b * (16 * C) + 16 * B)
                dve.tensor_copy(kmax[:], mem_max[:]).then_inc(state0, 1)
                dve.tensor_copy(zsum[:], mem_z[:]).then_inc(state0, 1)
                dve.tensor_copy(cacc[:], mem_ctx[:]).then_inc(state0, 1)
                hold(dve, state0, b * 4 + 3)

            def rest(b, c):
                n = dve.snap(b * C + c)
                k = dve.snap(b * (2 * C) + c)
                tile_stats(ht, k)
                dve.wait_ge(roots, k + 1)
                s6 = dve.snap(n * 6)
                dve.tensor_tensor(nrm[:], proot[:, 0, :], proot[:, 1, :], ALU.mult).then_inc(small, 1)
                dve.wait_ge(small, s6 + 1)
                dve.tensor_scalar(nrm[:], nrm[:], NORM_MIN / ROOT_E, None, ALU.max).then_inc(small, 1)
                dve.wait_ge(small, s6 + 2)
                dve.reciprocal(rnrm[:], nrm[:]).then_inc(small, 1)
                dve.wait_ge(small, s6 + 3)
                dve.tensor_tensor(scl[:], rnrm[:], proot[:, 0, :], ALU.mult).then_inc(small, 1)
                dve.tensor_scalar(sone[:], proot[:, 0, :], 1.0, None, ALU.add).then_inc(small, 1)
                dve.scalar_tensor_tensor(smean[:], mvar[:, :, 0], -1.0, proot[:, 0, :], ALU.mult, ALU.mult)\
                    .then_inc(small, 1)
                dve.wait_ge(small, s6 + 6)
                for t in range(TPC):
                    ins = dve.tensor_scalar(un[:, t, :], ht[:, t, :], mvar[:, t, 0:1], scl[:, t:t + 1],
                                            ALU.subtract, ALU.mult)
                ins.then_inc(un_ready, 1)
                dve.wait_ge(k_psum, n + 1)
                k2 = dve.snap(n * 2)
                dve.tensor_reduce(kchunk[:], p_k[:, 0:CH], AX.X, ALU.max).then_inc(kstep, 1)
                dve.wait_ge(kstep, k2 + 1)
                dve.tensor_tensor(knew[:], kmax[:], kchunk[:], ALU.max).then_inc(kstep, 1)
                dve.wait_ge(kstep, k2 + 2)
                dve.tensor_scalar(kneg[:], knew[:], -1.0, None, ALU.mult).then_inc(kneg_ready, 1)
                q3 = p_q[:, 0:CH].rearrange("p (g d) -> p g d", d=DH)
                qt3 = qt[:].rearrange("p t (g d) -> p (t g) d", d=DH)
                G = TPC * HEADS
                dve.wait_ge(q_psum, n + 1)
                q3n = dve.snap(n * 3)
                dve.tensor_reduce(qmax[:], q3, AX.X, ALU.max).then_inc(qstep, 1)
                dve.wait_ge(qstep, q3n + 1)
                dve.tensor_tensor(qt3, q3, qmax[:].unsqueeze(2).broadcast_to([P, G, DH]), ALU.subtract)\
                    .then_inc(qs_ready, 1)
                dve.wait_ge(q_exp, n + 1)
                dve.tensor_reduce(qsum[:], qt3, AX.X, ALU.add).then_inc(qstep, 1)
                dve.wait_ge(qstep, q3n + 2)
                dve.reciprocal(qsum[:], qsum[:]).then_inc(qstep, 1)
                dve.wait_ge(qstep, q3n + 3)
                dve.tensor_tensor(qt3, qt3, qsum[:].unsqueeze(2).broadcast_to([P, G, DH]), ALU.mult)\
                    .then_inc(qn_ready, 1)
                dve.wait_ge(ek_ready, n + 1)
                dve.tensor_copy(kmax[:], knew[:])
                dve.scalar_tensor_tensor(zsum[:], zsum[:], kcorr[:, 0:1], zchunk[:], ALU.mult, ALU.add)
                dve.wait_ge(c_psum, n + 1)
                dve.scalar_tensor_tensor(cacc[:], cacc[:], kcorr[:, 0:1], p_c[:, 0:P], ALU.mult, ALU.add)\
                    .then_inc(c_done, 1)
                dve.wait_ge(c_done, n + 1)

            def image(b, cp, par):
                c = dve.snap(cp * 2 + par)
                xi = dve.snap(b * CI + c)
                n = dve.snap(b * C + c)
                dve.wait_ge(tanh_ready, xi + 1)
                dve.scalar_tensor_tensor(slu[:], slu[:], 1.0, xc[par][:], ALU.add, ALU.mult)\
                    .then_inc(silu_ready, 1)
                dve.wait_ge(s_ready, n * TPC)
                dve.wait_ge(tok_psum, xi + 1)
                dve.tensor_tensor(ht[:], p_tok[:, 0:TPC * E].rearrange("p (t e) -> p t e", e=E),
                                  tok_bias[:].unsqueeze(1).broadcast_to([P, TPC, E]), ALU.add).then_inc(h_ready, 1)
                dve.wait_ge(h_ready, xi + 1)
                rest(b, c)

            def text(b, cp, par):
                dve.wait_ge(txt_in, b * (16 * CT) + cp * 32 + 16 * par + 16)
                rest(b, dve.snap(cp * 2 + par + CI))

            def out_(b):
                dve.reciprocal(zinv[:], zsum[:]).then_inc(state0, 1)
                dve.wait_ge(state0, b * 4 + 4)
                dve.scalar_tensor_tensor(cnorm[:], cacc[:], zinv[:, 0:1], head_mask[:], ALU.mult, ALU.mult)\
                    .then_inc(cn_ready, 1)
                with dve.Fori(0, C) as c:
                    n = dve.snap(b * C + c)
                    k = dve.snap(b * (2 * C) + C + c)
                    dve.wait_ge(y_psum, n + 1)
                    dve.tensor_tensor(yt[:], p_tok[:, 0:TPC * E].rearrange("p (t e) -> p t e", e=E),
                                      bo[:].unsqueeze(1).broadcast_to([P, TPC, E]), ALU.add).then_inc(y_ready, 1)
                    dve.wait_ge(ynorm, n + 1)
                    dve.tensor_scalar(nrm[:], nrm[:], NORM_MIN, None, ALU.max).then_inc(ysm, 1)
                    dve.wait_ge(ysm, n * 2 + 1)
                    dve.reciprocal(rnrm[:], nrm[:]).then_inc(ysm, 1)
                    dve.wait_ge(ysm, n * 2 + 2)
                    for t in range(TPC):
                        ins = dve.scalar_tensor_tensor(yt[:, t, :], yt[:, t, :], rnrm[:, t:t + 1], go[:],
                                                       ALU.mult, ALU.mult)
                    ins.then_inc(yg_ready, 1)
                    dve.wait_ge(h1_ready, n + 1)
                    tile_stats(ht, k)
                    dve.wait_ge(roots, k + 1)
                    for t in range(TPC):
                        ins = dve.tensor_scalar(un[:, t, :], ht[:, t, :], mvar[:, t, 0:1], proot[:, 0, t:t + 1],
                                                ALU.subtract, ALU.mult)
                    ins.then_inc(b_un, 1)

            with dve.Fori(0, B) as b:
                new_state(b)
                with dve.Fori(0, CI // 2) as cp:
                    for par in range(2):
                        image(b, cp, par)
                with dve.Fori(0, CT // 2) as cp:
                    for par in range(2):
                        text(b, cp, par)
                out_(b)


GATES = (2, 0, 1, 3)


def scan_phase(nc, ctx_outer, xr, ident, ones, inc_tot, args):
    w_hh, w_ih, b_ih, b_hh, w_lin, b_lin, fw, bw, h_dram, n_blocks, B = args
    COLS = B * U
    assert n_blocks % 2 == 0 and COLS == P
    G2 = 2

    with ExitStack() as ctx:
        def sb(name, shape, dt=F32):
            return ctx.enter_context(nc.sbuf_tensor(name, shape, dt))

        def sem(name):
            return ctx.enter_context(nc.semaphore(name))

        w1 = sb("w1", [P, HALVES, 8, P], F16)
        w2 = sb("w2", [P, HALVES, 8, P], F16)
        wih = sb("wih", [P, HALVES, 8, P])
        wst = wih
        brow = sb("brow", [1, 2, 8 * P])
        bsum = sb("bsum", [1, 8 * P])
        bpart = sb("bpart", [1, 3, 8 * P], F16)
        bias3 = sb("bias3", [3, 8 * P], F16)
        ones3 = sb("ones3", [3, COLS], F16)
        wlin = sb("wlin", [P, HALVES, 2])
        wdiff = sb("wdiff", [P, HALVES, P])
        wd1 = sb("wd1", [P, HALVES])
        blin = sb("blin", [P, 2])
        bdiff = sb("bdiff", [P, 1])
        fwt = sb("fwt", [P, HALVES])
        bwt = sb("bwt", [P, HALVES])
        nfw = sb("nfw", [P, HALVES])
        fmb = sb("fmb", [P, HALVES])
        hop = sb("hop", [P, 2, 2, HALVES, B], F16)
        gi = sb("gi", [P, HALVES, 2 * B])
        fo = sb("fo", [P, HALVES, 2, B, 2])
        cpair = sb("cpair", [P, HALVES, 2, 2 * B + 2])
        tc = sb("tc", [P, HALVES, B])
        hblk = [sb(f"hblk{i}", [P, HALVES, B, U]) for i in range(2)]
        mask = sb("mask", [P, COLS])
        wm = sb("wm", [P, HALVES, COLS])
        part = sb("part", [P, HALVES, COLS])
        inc = [sb(f"inc{i}", [P, HALVES, COLS]) for i in range(2)]
        inct = sb("inct", [P, HALVES, COLS])
        keep = sb("keep", [P, COLS])
        hres = sb("hres", [P, E])
        first_sig = sb("first_sig", [P, 1])

        gp = [[[ctx.enter_context(nc.psum_tensor(f"g{s}{h}{q}", [P, 512], F32)) for q in range(2)]
               for h in range(HALVES)] for s in range(2)]

        def gates(s, half, pair):
            return gp[s][half][pair][:, 0:G2 * COLS].rearrange("p (g b t) -> p g b t", g=G2, b=B)

        hold = holder(sem("held2"))
        lw = sem("lw")
        lw2 = sem("lw2")
        lw3 = sem("lw3")
        pre = sem("pre")
        pset = sem("pset")
        z0 = sem("z0")
        gi_psum = [sem("gi_psum0"), sem("gi_psum1")]
        fo_psum = [sem("fo_psum0"), sem("fo_psum1")]
        i_ready = [sem("i_ready0"), sem("i_ready1")]
        cin = [sem("cin0"), sem("cin1")]
        c_new = [sem("c_new0"), sem("c_new1")]
        tc_ready = [sem("tc_ready0"), sem("tc_ready1")]
        h1_out = [sem("h1_out0"), sem("h1_out1")]
        h_out = [sem("h_out0"), sem("h_out1")]
        h2_out = [sem("h2_out0"), sem("h2_out1")]
        x_psum = sem("x_psum")
        logit_psum = sem("logit_psum")
        mask_ready = sem("mask_ready")
        pstep = sem("pstep")
        wm_ready = sem("wm_ready")
        inc_ready = sem("inc_ready")
        part_ready = sem("part_ready")
        part_psum = sem("part_psum")
        res_in = sem("res_in")
        out_ready = sem("out_ready")
        PSTEPS = 7

        block = ctx.enter_context(nc.Block())

        @block.sync
        def _(sp):
            sp.dma_start(wst[:], w_hh).then_inc(lw, 16)
            sp.dma_start(brow[0:1, 0, :], b_ih).then_inc(lw2, 16)
            sp.dma_start(brow[0:1, 1, :], b_hh).then_inc(lw2, 16)
            sp.dma_start(wlin[:], w_lin).then_inc(lw2, 16)
            sp.dma_start(blin[:], b_lin.broadcast_to([P, 2])).then_inc(lw2, 16)
            sp.dma_start(fwt[:], fw).then_inc(lw2, 16)
            sp.dma_start(bwt[:], bw).then_inc(lw2, 16)
            sp.wait_ge(pre, 4)
            sp.dma_start(wih[:], w_ih).then_inc(lw3, 16)
            sp.wait_ge(pset, 3)
            for r in range(3):
                sp.dma_start(bias3[r:r + 1, :], bpart[0:1, r, :]).then_inc(lw3, 16)

            def residual(j):
                hold(sp, out_ready, j)
                sp.dma_start(hres[:], h_dram[:, bass.ds(j * U, U), :]).then_inc(res_in, 16)

            with sp.Fori(0, n_blocks // 2) as i:
                for s in range(2):
                    residual(sp.snap(i * 2 + s))
            residual(n_blocks)
            sp.wait_ge(res_in, 16 * (n_blocks + 1))

        @block.gpsimd
        def _(pool):
            for t in (hop, cpair, fo, hblk[1], inc[0], inc[1]):
                pool.memset(t[:], 0.0).then_inc(z0, 1)
            pool.memset(ones3[:], H_SCALE).then_inc(z0, 1)
            pool.memset(keep[:], 1.0).then_inc(z0, 1)
            pool.wait_ge(z0, 8)
            pool.memset(keep[:].rearrange("p (b t) -> p b t", b=B)[:, :, 0], 0.0).then_inc(z0, 1)
            pool.wait_ge(z0, 9)
            pool.wait_ge(pre, 10)

            def post(j, s):
                h = hblk[1 - s]
                hv = h[:].rearrange("p h b t -> p h (b t)")
                j7 = pool.snap(j * PSTEPS)
                pool.wait_ge(mask_ready, j + 1)
                pool.tensor_tensor(wm[:], hv, mask[:].unsqueeze(1).broadcast_to([P, HALVES, COLS]), ALU.mult)\
                    .then_inc(pstep, 1)
                for k in range(HALVES):
                    hold(pool, pstep, j7 + 1 + k)
                    pool.tensor_scalar(part[:, k, :], mask[:], nfw[:, k:k + 1], 2.0, ALU.mult, ALU.add)\
                        .then_inc(pstep, 1)
                pool.wait_ge(pstep, j7 + 3)
                pool.tensor_tensor(part[:], part[:], hv, ALU.mult).then_inc(pstep, 1)
                first = wm[:].rearrange("p h (b t) -> p h b t", b=B)[:, :, :, 0]
                last = inc[s][:].rearrange("p h (b t) -> p h b t", b=B)[:, :, :, U - 1]
                pool.wait_ge(inc_ready, j * HALVES)
                pool.tensor_tensor(first, first, last, ALU.add).then_inc(wm_ready, 1)
                hold(pool, inc_ready, j * HALVES + HALVES)
                for k in range(HALVES):
                    pool.tensor_scalar(inct[:, k, :], inc[1 - s][:, k, :], fmb[:, k:k + 1], None, ALU.mult)\
                        .then_inc(pstep, 1)
                pool.wait_ge(pstep, j7 + 6)
                pool.tensor_tensor(part[:], part[:], inct[:], ALU.add).then_inc(part_ready, 1)
                pool.wait_ge(part_ready, j + 1)
                pool.sem_inc(pstep, 1)

            with pool.Fori(0, n_blocks // 2) as i:
                for s in range(2):
                    post(pool.snap(i * 2 + s), s)
            post(n_blocks, 0)

        @block.scalar
        def _(act):
            act.wait_ge(z0, 9)
            act.activation(first_sig[:], keep[:, 0:1], ACT.Sigmoid)
            with act.Fori(0, n_blocks // 2) as i:
                base = act.snap(i * (2 * U))
                for s in range(2):
                    for t in range(U):
                        step = s * U + t
                        nxt = 1 - step % 2

                        def gate_gi(h):
                            act.wait_ge(gi_psum[h], base + step + 1)
                            act.activation(gi[:, h, 0:B], gates(s, h, 0)[:, 0, :, t], ACT.Tanh, scale=1.0 / GATE_SCALE)
                            act.activation(gi[:, h, B:2 * B], gates(s, h, 0)[:, 1, :, t], ACT.Sigmoid,
                                           scale=1.0 / GATE_SCALE).then_inc(i_ready[h], 1)

                        def gate_fo(h):
                            act.wait_ge(fo_psum[h], base + step + 1)
                            act.activation(fo[:, h, :, :, 1], gates(s, h, 1)[:, :, :, t], ACT.Sigmoid,
                                           scale=1.0 / GATE_SCALE).then_inc(cin[h], 1)

                        def tanh_c(h):
                            act.wait_ge(c_new[h], base + step + 1)
                            act.activation(tc[:, h, :], cpair[:, h, nxt, 1:2 * B:2], ACT.Tanh)\
                                .then_inc(tc_ready[h], 1)

                        gate_gi(0)
                        gate_fo(0)
                        gate_gi(1)
                        gate_fo(1)
                        tanh_c(0)
                        tanh_c(1)

        @block.tensor
        def _(pe):
            pe.wait_ge(z0, 9)
            pe.wait_ge(pre, 10)
            pe.wait_ge(lw3, 64)

            def x_bias(s, half, pair, g):
                m = half * 4 + pair * 2 + g
                pe.matmul(gates(s, half, pair)[:, g, :, :].rearrange("p b t -> p (b t)"),
                          bias3[:, m * P:(m + 1) * P], ones3[:], start=(g == 0), stop=False, skip_group_check=True)

            def x_part(s, half, pair, g, kc, j):
                m = half * 4 + pair * 2 + g
                return pe.matmul(gates(s, half, pair)[:, g, :, :].rearrange("p b t -> p (b t)"), wih[:, kc, m, :],
                                 xr[:, bass.ds(j + 1, 1), kc, :, :].rearrange("p k b t -> p (k b t)"),
                                 start=False, stop=False, skip_group_check=True)

            slots = [(half, pair, g, kc) for half in range(HALVES) for pair in range(2) for g in range(2)
                     for kc in range(HALVES)]

            def logits(s, kc):
                mm = pe.matmul(gp[1 - s][0][0][:, G2 * COLS:G2 * COLS + COLS], wdiff[:, kc, :],
                               hblk[1 - s][:, kc, :, :].rearrange("p b t -> p (b t)"),
                               start=(kc == 0), stop=(kc == HALVES - 1), skip_group_check=True)
                if kc == HALVES - 1:
                    mm.then_inc(logit_psum, 1)

            def turn(s, j):
                pe.wait_ge(part_ready, j + 1)
                for k in range(HALVES):
                    mm = pe.transpose(gp[1 - s][0][1][:, G2 * COLS + k * P:G2 * COLS + (k + 1) * P],
                                      part[:, k, :], ident[:])
                mm.then_inc(part_psum, 1)

            for half, pair, g, kc in slots:
                if kc == 0:
                    x_bias(0, half, pair, g)
                x_part(0, half, pair, g, kc, 0)

            PASSES = ((w2, 0, h1_out), (w1, 0, h1_out), (w1, 1, h2_out))
            EARLY = ((0, 0), (0, 1), (0, 2), (1, 0), (1, 1), (1, 2), (1, 3))

            with pe.Fori(0, n_blocks // 2) as i:
                base = pe.snap(i * (2 * U))
                for s in range(2):
                    j = pe.snap(i * 2 + s)
                    for t in range(U):
                        step = s * U + t
                        par = step % 2

                        def mm(wt, hp, kc, half, m):
                            return pe.matmul(gates(s, half, m // 2)[:, m % 2, :, t], wt[:, kc, half * 4 + m, :],
                                             hop[:, par, hp, kc, :], start=False, stop=False,
                                             skip_group_check=True)

                        for wt, hp, ready in PASSES:
                            if wt is not w1 or hp:
                                pe.wait_ge(ready[0], base + step)
                            for half, m in EARLY:
                                mm(wt, hp, 0, half, m)
                        for wt, hp, ready in PASSES:
                            if wt is not w1 or hp:
                                pe.wait_ge(ready[1], base + step)
                            for m in range(2):
                                last = mm(wt, hp, 1, 0, m)
                        last.then_inc(gi_psum[0], 1)
                        for wt, hp, _ in PASSES:
                            mm(wt, hp, 0, 0, 3)
                        for wt, hp, _ in PASSES:
                            for m in range(2, 4):
                                last = mm(wt, hp, 1, 0, m)
                        last.then_inc(fo_psum[0], 1)
                        for pair, done in ((0, gi_psum), (1, fo_psum)):
                            for wt, hp, _ in PASSES:
                                for m in range(2 * pair, 2 * pair + 2):
                                    last = mm(wt, hp, 1, 1, m)
                            last.then_inc(done[1], 1)
                        if t < HALVES:
                            logits(s, t)
                        if t == 12:
                            turn(s, j)
                        if t == 15:
                            pe.wait_ge(out_ready, j + 1)
                        if 15 <= t < 15 + len(slots):
                            half, pair, g, kc = slots[t - 15]
                            if kc == 0:
                                x_bias(1 - s, half, pair, g)
                            x_part(1 - s, half, pair, g, kc, j + 1)
            for h in range(HALVES):
                pe.wait_ge(h2_out[h], n_blocks * U)
            logits(0, 0)
            logits(0, 1)
            turn(0, n_blocks)

        @block.vector
        def _(dve):
            flat = "p h m c -> p (h m c)"
            dve.wait_ge(lw, 16)
            dve.tensor_scalar(wst[:].rearrange(flat), wst[:].rearrange(flat), W_SCALE, None, ALU.mult).then_inc(pre, 1)
            dve.wait_ge(pre, 1)
            dve.tensor_copy(w1[:].rearrange(flat), wst[:].rearrange(flat)).then_inc(pre, 1)
            dve.wait_ge(pre, 2)
            dve.tensor_tensor(w2[:].rearrange(flat), wst[:].rearrange(flat), w1[:].rearrange(flat), ALU.subtract)\
                .then_inc(pre, 1)
            dve.wait_ge(pre, 3)
            dve.sem_inc(pre, 1)
            dve.wait_ge(lw2, 96)
            dve.tensor_tensor(bsum[:], brow[0:1, 0, :], brow[0:1, 1, :], ALU.add).then_inc(pset, 1)
            dve.wait_ge(pset, 1)
            dve.tensor_scalar(bsum[:], bsum[:], W_SCALE, None, ALU.mult).then_inc(pset, 1)
            dve.wait_ge(pset, 2)
            bs = sem("bs")
            dve.tensor_copy(bpart[0:1, 0, :], bsum[:]).then_inc(bs, 1)
            dve.wait_ge(bs, 1)
            dve.tensor_tensor(bsum[:], bsum[:], bpart[0:1, 0, :], ALU.subtract).then_inc(bs, 1)
            dve.wait_ge(bs, 2)
            dve.tensor_copy(bpart[0:1, 1, :], bsum[:]).then_inc(bs, 1)
            dve.wait_ge(bs, 3)
            dve.tensor_tensor(bsum[:], bsum[:], bpart[0:1, 1, :], ALU.subtract).then_inc(bs, 1)
            dve.wait_ge(bs, 4)
            dve.tensor_copy(bpart[0:1, 2, :], bsum[:]).then_inc(pset, 1)
            dve.tensor_tensor(wd1[:], wlin[:, :, 1], wlin[:, :, 0], ALU.subtract).then_inc(pre, 1)
            dve.wait_ge(pre, 5)
            dve.tensor_copy(wdiff[:], wd1[:].unsqueeze(2).broadcast_to([P, HALVES, P])).then_inc(pre, 1)
            dve.tensor_tensor(bdiff[:], blin[:, 1:2], blin[:, 0:1], ALU.subtract).then_inc(pre, 1)
            dve.tensor_scalar(nfw[:], fwt[:], -1.0, None, ALU.mult).then_inc(pre, 1)
            dve.tensor_tensor(fmb[:], fwt[:], bwt[:], ALU.subtract).then_inc(pre, 1)
            dve.wait_ge(lw3, 64)
            dve.tensor_scalar(wih[:].rearrange(flat), wih[:].rearrange(flat), GATE_SCALE, None, ALU.mult).then_inc(pre, 1)
            dve.wait_ge(z0, 9)
            dve.wait_ge(pre, 10)

            def to_mask(s, j):
                dve.wait_ge(logit_psum, j + 1)
                dve.tensor_scalar(mask[:], gp[1 - s][0][0][:, G2 * COLS:G2 * COLS + COLS], bdiff[:, 0:1], 0.0,
                                  ALU.add, ALU.is_gt).then_inc(mask_ready, 1)

            def run_sum(s, j, k):
                dve.wait_ge(wm_ready, j + 1)
                dve.tensor_tensor_scan(inc[1 - s][:, k, :], keep[:], wm[:, k, :], 0.0, ALU.mult, ALU.add)\
                    .then_inc(inc_ready, 1)

            def add_residual(s, j):
                dve.wait_ge(res_in, j * 16 + 16)
                dve.wait_ge(part_psum, j + 1)
                dve.tensor_tensor(xr[:, bass.ds(j, 1), :, :, :].rearrange("p k h b t -> p (k h b t)"),
                                  gp[1 - s][0][1][:, G2 * COLS:G2 * COLS + E], hres[:], ALU.add)\
                    .then_inc(out_ready, 1)

            with dve.Fori(0, n_blocks // 2) as i:
                base = dve.snap(i * (2 * U))
                base2 = dve.snap(i * (4 * U))
                for s in range(2):
                    j = dve.snap(i * 2 + s)
                    for t in range(U):
                        step = s * U + t
                        par, nxt = step % 2, 1 - step % 2

                        def i_times_g(h):
                            dve.wait_ge(i_ready[h], base + step + 1)
                            dve.tensor_tensor(cpair[:, h, par, 2:2 * B + 2:2], gi[:, h, 0:B], gi[:, h, B:2 * B],
                                              ALU.mult).then_inc(cin[h], 1)

                        def new_c(h):
                            dve.wait_ge(cin[h], base2 + 2 * step + 2)
                            dve.tensor_tensor_scan(cpair[:, h, nxt, 0:2 * B],
                                                   fo[:, h, 0, :, :].rearrange("p b two -> p (b two)"),
                                                   cpair[:, h, par, 1:2 * B + 1], 0.0, ALU.mult, ALU.add)\
                                .then_inc(c_new[h], 1)

                        def new_h(h):
                            o = fo[:, h, 1, :, 1]
                            dve.wait_ge(tc_ready[h], base + step + 1)
                            dve.scalar_tensor_tensor(hop[:, nxt, 0, h, :], o, H_SCALE, tc[:, h, :], ALU.mult, ALU.mult)\
                                .then_inc(h1_out[h], 1)
                            dve.tensor_tensor(hblk[s][:, h, :, t], o, tc[:, h, :], ALU.mult).then_inc(h_out[h], 1)

                        def rest_h(h):
                            dve.wait_ge(h_out[h], base + step + 1)
                            dve.scalar_tensor_tensor(hop[:, nxt, 1, h, :], hblk[s][:, h, :, t], H_SCALE,
                                                     hop[:, nxt, 0, h, :], ALU.mult, ALU.subtract)\
                                .then_inc(h2_out[h], 1)

                        i_times_g(0)
                        new_c(0)
                        i_times_g(1)
                        new_c(1)
                        new_h(0)
                        rest_h(0)
                        new_h(1)
                        rest_h(1)
                        if t == 2:
                            to_mask(s, j)
                        if t in (7, 8):
                            run_sum(s, j, t - 7)
                        if t == 14:
                            add_residual(s, j)
            to_mask(0, n_blocks)
            run_sum(0, n_blocks, 0)
            run_sum(0, n_blocks, 1)
            add_residual(0, n_blocks)
            dve.wait_ge(inc_ready, (n_blocks + 1) * HALVES)
            total = inc[1][:].rearrange("p h (b t) -> p h b t", b=B)[:, :, :, U - 1:U]
            for k in range(HALVES):
                dve.tensor_scalar(inc_tot[:, k, :].rearrange("p (b t) -> p b t", b=B),
                                  total[:, k, :, :].broadcast_to([P, B, U]), bwt[:, k:k + 1], None, ALU.mult)


def suffix_phase(nc, xr, ident, inc_tot, out, n_blocks, B):
    K = 8
    assert n_blocks % K == 0
    with ExitStack() as ctx:
        tot = ctx.enter_context(nc.sbuf_tensor("tot", [P, E], F32))
        ps = ctx.enter_context(nc.psum_tensor("ps", [P, 512], F32))
        tot_psum = ctx.enter_context(nc.semaphore("tot_psum"))
        tot_ready = ctx.enter_context(nc.semaphore("tot_ready"))
        done = ctx.enter_context(nc.semaphore("done"))
        stored = ctx.enter_context(nc.semaphore("stored"))
        N = n_blocks // K
        block = ctx.enter_context(nc.Block())

        @block.tensor
        def _(pe):
            for k in range(HALVES):
                mm = pe.transpose(ps[:, k * P:(k + 1) * P], inc_tot[:, k, :], ident[:])
            mm.then_inc(tot_psum, 1)

        @block.vector
        def _(dve):
            dve.wait_ge(tot_psum, 1)
            dve.tensor_copy(tot[:], ps[:, 0:E]).then_inc(tot_ready, 1)
            dve.wait_ge(tot_ready, 1)
            with dve.Fori(0, N) as i:
                blk = xr[:, bass.ds(i * K + 1, K), :, :, :].rearrange("p k h b t -> p k (h b t)")
                dve.tensor_tensor(blk, blk, tot[:].unsqueeze(1).broadcast_to([P, K, E]), ALU.add).then_inc(done, 1)

        @block.sync
        def _(sp):
            with sp.Fori(0, N) as i:
                sp.wait_ge(done, i + 1)
                for b in range(B):
                    sp.dma_start(out[b, bass.ds(i * (K * U), K * U), :].rearrange("(k t) d -> t k d", t=U),
                                 xr[b * U:(b + 1) * U, bass.ds(i * K + 1, K), :, :, :]
                                 .rearrange("p k h b t -> p k (h b t)")).then_inc(stored, 16)
            sp.wait_ge(stored, 16 * B * N)


def build(nc, x, txt, bases, w_spline, b_spline, w_base, b_base, w_qkv, mem_k, mem_v, w_out, b_out, g_out, g_pre,
          w_ih, w_hh, b_ih, b_hh, w_lin, b_lin, fw, bw, out):
    B = x.shape[0]
    T = x.shape[2] + txt.shape[1]
    n_blocks = T // U
    s_dram = nc.dram_tensor("s_rows", (B, T, E), F32, kind="Internal").ap()
    h_dram = nc.dram_tensor("h_rows", (B, U + T, E), F32, kind="Internal").ap()
    with ExitStack() as ctx:
        xr = ctx.enter_context(nc.sbuf_tensor("xr", [P, n_blocks + 2, HALVES, B, U], F32))
        ident = ctx.enter_context(nc.sbuf_tensor("ident", [P, P], F32))
        ones = ctx.enter_context(nc.sbuf_tensor("ones", [P, P], F32))
        inc_tot = ctx.enter_context(nc.sbuf_tensor("inc_tot", [P, HALVES, B * U], F32))
        token_phases(nc, ctx, xr, ident, ones,
                     (x, txt, bases, w_spline, b_spline, w_base, b_base, w_qkv, mem_k, mem_v, w_out, b_out, g_out,
                      g_pre, s_dram, h_dram))
        scan_phase(nc, ctx, xr, ident, ones, inc_tot,
                   (w_hh, w_ih, b_ih, b_hh, w_lin, b_lin, fw, bw, h_dram, n_blocks, B))
        suffix_phase(nc, xr, ident, inc_tot, out, n_blocks, B)


def layout(inputs):
    import numpy as np
    a = {k: np.asarray(v) for k, v in inputs.items()}
    x = a["x"]
    B, C = x.shape[0], x.shape[1]

    def rows(w):
        return np.ascontiguousarray(w.reshape(HALVES, P, -1).transpose(1, 0, 2))

    def gate_tiles(w):
        v = w.reshape(4, HALVES, P, HALVES, P)[list(GATES)]
        return np.ascontiguousarray(v.transpose(4, 3, 1, 0, 2).reshape(P, HALVES, 8, P))

    def gate_row(b):
        return np.ascontiguousarray(b.reshape(4, HALVES, P)[list(GATES)].transpose(1, 0, 2).reshape(1, 8 * P))

    return {
        "x": np.ascontiguousarray(x.reshape(B, C, -1)),
        "txt": np.ascontiguousarray(a["txt"]),
        "bases": rows(a["L0_tok_bases"]),
        "w_spline": np.ascontiguousarray(a["L0_tok_W_spline"].T.reshape(HALVES, P, NB, E).transpose(1, 2, 0, 3)),
        "b_spline": a["L0_tok_b_spline"].reshape(1, E),
        "w_base": rows(a["L0_tok_W_base"].T),
        "b_base": a["L0_tok_b_base"].reshape(1, E),
        "w_qkv": rows(a["L0_attn_w_qkv"]),
        "mem_k": np.ascontiguousarray(a["L0_attn_mem_kv"][0].reshape(P, MEM)),
        "mem_v": np.ascontiguousarray(a["L0_attn_mem_kv"][1].reshape(P, MEM).T),
        "w_out": np.ascontiguousarray(a["L0_attn_w_out"]),
        "b_out": a["L0_attn_b_out"].reshape(1, E),
        "g_out": a["L0_attn_g_out"].reshape(1, E),
        "g_pre": np.ascontiguousarray(a["L0_attn_g_pre"].reshape(HALVES, P).T),
        "w_ih": gate_tiles(a["L0_ffn_W_ih"]),
        "w_hh": gate_tiles(a["L0_ffn_W_hh"]),
        "b_ih": gate_row(a["L0_ffn_b_ih"]),
        "b_hh": gate_row(a["L0_ffn_b_hh"]),
        "w_lin": rows(a["L0_ffn_W_lin"].T),
        "b_lin": a["L0_ffn_b_lin"].reshape(1, 2),
        "fw": np.ascontiguousarray(a["L0_ffn_fw_att"].reshape(HALVES, P).T),
        "bw": np.ascontiguousarray(a["L0_ffn_bw_att"].reshape(HALVES, P).T),
    }


def kernel(**inputs):
    import concourse.bacc as bacc
    from concourse.bass_utils import run_bass_kernel_spmd

    arrays = layout(inputs)
    B, T = arrays["x"].shape[0], arrays["x"].shape[2] + arrays["txt"].shape[1]
    nc = bacc.Bacc("TRN2", target_bir_lowering=False, num_devices=1)
    args = [nc.dram_tensor(name, a.shape, mybir.dt.from_np(a.dtype), kind="ExternalInput").ap()
            for name, a in arrays.items()]
    args.append(nc.dram_tensor("out", (B, T, E), F32, kind="ExternalOutput").ap())
    build(nc, *args)
    return run_bass_kernel_spmd(nc, [arrays], core_ids=[0]).results[0]["out"]
```

```python
import concourse.bass as bass
from concourse import mybir
from contextlib import ExitStack

F32 = mybir.dt.float32
F16 = mybir.dt.float16
ALU = mybir.AluOpType
ACT = mybir.ActivationFunctionType
AX = mybir.AxisListType

P = 128
E = 256
HALVES = E // P
HEADS, DH, MEM = 4, 32, 4
NB = 3
CH = 256
TPC = CH // P
U = 32
LN_EPS = 1e-5
NORM_MIN = 1e-12
ROOT_E = float(E) ** 0.5

W_SCALE = 2.0 ** 9
H_SCALE = 2.0 ** 10
GATE_SCALE = W_SCALE * H_SCALE


def number(engine, b, value):
    return engine.snap(b * 0 + value)


FIRST = 1


def holder(held):
    def hold(engine, semaphore, value):
        engine.wait_ge(semaphore, value)
        engine.sem_inc(held, 1)
    return hold


def token_phases(nc, ctx_outer, xr, ident, ones, args):
    (x, txt, bases, w_spline, b_spline, w_base, b_base, w_qkv, mem_k, mem_v, w_out, b_out, g_out,
     g_pre, s_dram, h_dram) = args
    B = x.shape[0]
    n_img = x.shape[2]
    n_txt = txt.shape[1]
    CI = n_img // CH
    CT = n_txt // CH
    C = CI + CT
    BPC = CH // U
    assert CI % 2 == 0 and CT % 2 == 0

    with ExitStack() as ctx:
        def sb(name, shape, dt=F32):
            return ctx.enter_context(nc.sbuf_tensor(name, shape, dt))

        def pb(name):
            return ctx.enter_context(nc.psum_tensor(name, [P, 512], F32))

        def sem(name):
            return ctx.enter_context(nc.semaphore(name))

        wsp = sb("wsp", [P, NB, HALVES, E])
        wba = sb("wba", [P, HALVES, E])
        wqkv = sb("wqkv", [P, HALVES, 3 * P])
        wo = sb("wo", [P, E])
        hbase = sb("hbase", [P, HALVES, NB])
        gpre = sb("gpre", [P, HALVES])
        bias_rows = sb("bias_rows", [1, 2, E])
        tok_bias = sb("tok_bias", [P, E])
        bo = sb("bo", [P, E])
        go = sb("go", [P, E])
        mk = sb("mk", [P, MEM])
        mv = sb("mv", [MEM, P])
        head_mask = sb("head_mask", [P, P])
        expo = sb("expo", [P, 2, TPC])
        eps2 = sb("eps2", [P, 2, TPC])
        mem_max = sb("mem_max", [P, 1])
        mem_neg = sb("mem_neg", [P, 1])
        mem_e = sb("mem_e", [P, MEM])
        mem_eT = sb("mem_eT", [MEM, P])
        mem_z = sb("mem_z", [P, 1])
        mem_ctx = sb("mem_ctx", [P, P])
        kmax = sb("kmax", [P, 1])
        knew = sb("knew", [P, 1])
        kchunk = sb("kchunk", [P, 1])
        kneg = sb("kneg", [P, 1])
        kcorr = sb("kcorr", [P, 1])
        zsum = sb("zsum", [P, 1])
        zchunk = sb("zchunk", [P, 1])
        zinv = sb("zinv", [P, 1])
        cacc = sb("cacc", [P, P])
        cnorm = sb("cnorm", [P, P])
        cT = sb("cT", [P, P])
        cw = sb("cw", [P, E])
        xc = [sb(f"xc{i}", [P, HALVES, CH]) for i in range(2)]
        spl = sb("spl", [P, NB, HALVES, CH])
        slu = sb("slu", [P, HALVES, CH])
        ht = sb("ht", [P, TPC, E])
        un = sb("un", [P, TPC, E])
        unT = sb("unT", [P, HALVES, CH])
        st = sb("st", [P, TPC, E])
        vt = sb("vt", [P, TPC, P])
        ek = sb("ek", [P, CH])
        ekT = sb("ekT", [P, TPC, P])
        qt = sb("qt", [P, TPC, P])
        yt = sb("yt", [P, TPC, E])
        stats = sb("stats", [P, TPC, 6])
        mvar = sb("mvar", [P, TPC, 2])
        vroot = sb("vroot", [P, 2, TPC])
        proot = sb("proot", [P, 2, TPC])
        nrm = sb("nrm", [P, TPC])
        rnrm = sb("rnrm", [P, TPC])
        scl = sb("scl", [P, TPC])
        sone = sb("sone", [P, TPC])
        smean = sb("smean", [P, TPC])
        qmax = sb("qmax", [P, TPC * HEADS])
        qsum = sb("qsum", [P, TPC * HEADS])
        sumsq = sb("sumsq", [P, TPC])

        p_tok = [pb("p_tok0"), pb("p_tok1")]
        p_uT, p_k, p_q, p_v, p_qT, p_c = [pb(n) for n in ("p_uT", "p_k", "p_q", "p_v", "p_qT", "p_c")]
        p_e = p_c[:, CH:2 * CH]
        y_of = [yt, slu]
        squares = spl[:, 0]
        s_of = [st, spl[:, 2]]
        h1_of = [ht, xc[0]]
        qTt = [spl[:, 1, 0, :], spl[:, 1, 1, :]]

        hold = holder(sem("held"))
        weights_in = sem("weights_in")
        consts = sem("consts")
        prep = sem("prep")
        bias_psum = sem("bias_psum")
        mem_exp = sem("mem_exp")
        mem_tr = sem("mem_tr")
        mem_trs = sem("mem_trs")
        mem_c = sem("mem_c")
        setup_done = sem("setup_done")
        x_in = [sem("x_in0"), sem("x_in1")]
        txt_in = sem("txt_in")
        tanh_ready = sem("tanh_ready")
        silu_ready = sem("silu_ready")
        tok_psum = [sem(f"tok_psum{t}") for t in range(TPC)]
        h_ready = [sem(f"h_ready{t}") for t in range(TPC)]
        stat_a = sem("stat_a")
        stat_b = sem("stat_b")
        roots_in = sem("roots_in")
        roots = sem("roots")
        small = sem("small")
        un_ready = sem("un_ready")
        s_ready = sem("s_ready")
        s_stored = sem("s_stored")
        uT_psum = sem("uT_psum")
        uT_ready = sem("uT_ready")
        k_psum = sem("k_psum")
        q_psum = sem("q_psum")
        v_psum = sem("v_psum")
        kstep = sem("kstep")
        kneg_ready = sem("kneg_ready")
        ek_ready = sem("ek_ready")
        e_psum = sem("e_psum")
        eT_ready = sem("eT_ready")
        v_ready = sem("v_ready")
        qstep = sem("qstep")
        qs_ready = sem("qs_ready")
        q_exp = sem("q_exp")
        qn_ready = sem("qn_ready")
        qT_psum = sem("qT_psum")
        qT_ready = sem("qT_ready")
        c_psum = sem("c_psum")
        c_done = sem("c_done")
        state0 = sem("state0")
        cn_ready = sem("cn_ready")
        cT_psum = sem("cT_psum")
        cT_ready = sem("cT_ready")
        cw_psum = sem("cw_psum")
        cw_ready = sem("cw_ready")
        s_in = [sem("s_in0"), sem("s_in1")]
        qT_back = sem("qT_back")
        y_psum = sem("y_psum")
        y_ready = sem("y_ready")
        sq_ready = sem("sq_ready")
        ynorm = sem("ynorm")
        ysm = sem("ysm")
        yg_ready = sem("yg_ready")
        h1_ready = sem("h1_ready")
        zeros_stored = sem("zeros_stored")
        h1_stored = [sem("h1_stored0"), sem("h1_stored1")]
        b_un = sem("b_un")
        b_uT = sem("b_uT")
        xr_ready = sem("xr_ready")

        def slots(c, b, half):
            v = xr[:, bass.ds(c * BPC + 1, BPC), half, bass.ds(b, 1), :]
            return v.rearrange("p k a s -> p k (a s)")

        def chunk_steps(e, b, step):
            step(b, -1, back=False, mid=False, front="image", par=0)
            step(b, 0, back=False, mid=True, front="image", par=1)
            with e.Fori(0, (CI - 2) // 2) as i:
                for par in range(2):
                    step(b, e.snap(i * 2 + 1 + par), back=True, mid=True, front="image", par=par)
            for m in range(CI - 1, C + 1):
                step(b, m, back=True, mid=m < C, front="text" if m < C - 1 else None, par=0)

        def out_steps(e, b, step):
            step(b, -2, back=False, mid=False, front=False, ahead=True, par=1)
            step(b, -1, back=False, mid=False, front=True, ahead=True, par=0)
            step(b, 0, back=False, mid=True, front=True, ahead=True, par=1)
            with e.Fori(0, (C - 4) // 2) as i:
                for par in range(2):
                    step(b, e.snap(i * 2 + 1 + par), back=True, mid=True, front=True, ahead=True, par=par)
            for m in range(C - 3, C + 1):
                step(b, m, back=True, mid=m < C, front=m < C - 1, ahead=m < C - 2, par=(m + 1) % 2)

        block = ctx.enter_context(nc.Block())

        @block.sync
        def _(sp):
            for dst, src in ((wsp, w_spline), (wba, w_base), (wqkv, w_qkv), (wo, w_out), (hbase, bases),
                             (gpre, g_pre), (mk, mem_k), (mv, mem_v)):
                sp.dma_start(dst[:], src).then_inc(weights_in, 16)
            sp.dma_start(bias_rows[0:1, 0, :], b_spline).then_inc(weights_in, 16)
            sp.dma_start(bias_rows[0:1, 1, :], b_base).then_inc(weights_in, 16)
            sp.dma_start(bo[:], b_out.broadcast_to([P, E])).then_inc(weights_in, 16)
            sp.dma_start(go[:], g_out.broadcast_to([P, E])).then_inc(weights_in, 16)
            sp.wait_ge(consts, 1)
            for b in range(B):
                sp.dma_start(h_dram[b, 0:U, :], st[0:U, 0, :]).then_inc(zeros_stored, 16)
            sp.wait_ge(zeros_stored, 16 * B)

            def load_x(b, c, par):
                xi = sp.snap(b * CI + c)
                hold(sp, silu_ready, xi * TPC + TPC)
                sp.dma_start(xc[par][:], x[bass.ds(b, 1), :, bass.ds(c * CH, CH)]
                             .rearrange("a (h p) n -> p (a h) n", p=P)).then_inc(x_in[par], 16)

            def step(b, m, back, mid, front, par):
                if front == "image":
                    load_x(b, number(sp, b, m + 1), par)
                if back:
                    c = number(sp, b, m - 1)
                    hold(sp, s_ready, sp.snap(b * C + c) * TPC + TPC + FIRST)
                    sp.dma_start(s_dram[bass.ds(b, 1), bass.ds(c * CH, CH), :]
                                 .rearrange("a (t p) d -> p (a t) d", p=P), st[:]).then_inc(s_stored, 16)
                if front == "text":
                    n = sp.snap(b * C + m + 1)
                    hold(sp, un_ready, n + FIRST)
                    hold(sp, s_ready, n * TPC + FIRST)
                    sp.dma_start(ht[:], txt[bass.ds(b, 1), (m + 1 - CI) * CH:(m + 2 - CI) * CH, :]
                                 .rearrange("a (t p) d -> p (a t) d", p=P)).then_inc(txt_in, 16)

            with sp.Fori(0, B) as b:
                chunk_steps(sp, b, step)
                hold(sp, s_stored, b * (16 * C) + 16 * C + FIRST)

                def load_s(c, q, wait):
                    if wait:
                        hold(sp, h1_ready, sp.snap(b * C + c) - 1 + FIRST)
                    sp.dma_start(s_of[q][:], s_dram[bass.ds(b, 1), bass.ds(c * CH, CH), :]
                                 .rearrange("a (t p) d -> p (a t) d", p=P)).then_inc(s_in[q], 16)

                def store_h1(c, q):
                    hold(sp, h1_ready, b * C + c + 1 + FIRST)
                    sp.dma_start(h_dram[bass.ds(b, 1), bass.ds(c * CH + U, CH), :]
                                 .rearrange("a (t p) d -> p (a t) d", p=P), h1_of[q][:]).then_inc(h1_stored[q], 16)

                load_s(0, 0, False)
                load_s(1, 1, False)
                store_h1(0, 0)
                with sp.Fori(0, (C - 2) // 2) as i:
                    for q in range(2):
                        load_s(sp.snap(i * 2 + 2 + q), q, True)
                        store_h1(sp.snap(i * 2 + 1 + q), 1 - q)
                store_h1(C - 1, 1)
                for q in range(2):
                    hold(sp, h1_stored[q], b * (8 * C) + 8 * C + FIRST)
                hold(sp, b_un, b * C + C + FIRST)

        @block.gpsimd
        def _(pool):
            for start in (h1_ready, s_stored, b_un, c_done, y_ready, xr_ready, s_ready, b_uT, un_ready,
                          *h1_stored, *tok_psum, *h_ready):
                pool.sem_inc(start, FIRST)
            pool.memset(st[:], 0.0).then_inc(consts, 1)
            pool.memset(ident[:], 0.0).then_inc(consts, 1)
            pool.memset(ones[:], 1.0).then_inc(consts, 1)
            pool.memset(head_mask[:], 0.0).then_inc(consts, 1)
            pool.memset(xr[:, xr.shape[1] - 1, :, :, :], 0.0).then_inc(consts, 1)
            pool.memset(expo[:, 0, :], -0.5).then_inc(consts, 1)
            pool.memset(expo[:, 1, :], 0.5).then_inc(consts, 1)
            pool.memset(eps2[:, 0, :], LN_EPS).then_inc(consts, 1)
            pool.memset(eps2[:, 1, :], 0.0).then_inc(consts, 1)
            pool.wait_ge(consts, 9)
            pool.affine_select(out=ident[:], in_=ident[:], compare_op=ALU.not_equal, fill=1.0, base=0,
                               pattern=[[-1, P]], channel_multiplier=1).then_inc(consts, 1)
            for h in range(HEADS):
                pool.wait_ge(consts, 10 + h)
                pool.memset(head_mask[h * DH:(h + 1) * DH, h * DH:(h + 1) * DH], float(DH) ** -0.5)\
                    .then_inc(consts, 1)
            pool.wait_ge(consts, 10 + HEADS)
            pool.wait_ge(zeros_stored, 16 * B)

            def roots_of(n):
                pool.wait_ge(roots_in, n + 1)
                pool.tensor_tensor(proot[:], vroot[:], expo[:], ALU.pow).then_inc(roots, 1)

            def out_step(b, m, back, mid, front, ahead, par):
                n = pool.snap(b * C + m)
                if mid:
                    q = 1 - par
                    hold(pool, s_in[q], b * (8 * C) + m * 8 + (16 - 8 * q))
                    hold(pool, h1_stored[q], b * (8 * C) + m * 8 + (FIRST - 8 * q))
                    hold(pool, yg_ready, n + 1)
                    if back:
                        hold(pool, b_un, n - 1 + FIRST)
                    pool.tensor_tensor(h1_of[q][:], y_of[q][:], s_of[q][:], ALU.add).then_inc(h1_ready, 1)
                if front:
                    pool.wait_ge(sq_ready, n + 2)
                    pool.tensor_tensor(nrm[:], sumsq[:], expo[:, 1, :], ALU.pow).then_inc(ynorm, 1)
                if mid:
                    roots_of(pool.snap(b * (2 * C) + C + m))

            with pool.Fori(0, B) as b:
                with pool.Fori(0, C) as c:
                    n = pool.snap(b * C + c)
                    roots_of(pool.snap(b * (2 * C) + c))
                    pool.wait_ge(s_stored, n * 16 + FIRST)
                    hold(pool, small, n * 6 + 6)
                    for t in range(TPC):
                        pool.tensor_scalar(st[:, t, :], ht[:, t, :], sone[:, t:t + 1], smean[:, t:t + 1],
                                           ALU.mult, ALU.add).then_inc(s_ready, 1)
                out_steps(pool, b, out_step)

        @block.scalar
        def _(act):
            act.wait_ge(prep, 6)
            act.activation(mem_e[:], mk[:], ACT.Exp, bias=mem_neg[:, 0:1], accum_out=mem_z[:, 0:1])\
                .then_inc(mem_exp, 1)

            def step(b, m, back, mid, front, par):
                n = act.snap(b * C + m)
                if front == "image":
                    c = number(act, b, m + 1)
                    xi = act.snap(b * CI + m + 1)
                    hold(act, x_in[par], b * (8 * CI) + c * 8 + (16 - 8 * par))
                    for t in range(TPC):
                        tok = slice(t * P, (t + 1) * P)
                        act.wait_ge(tok_psum[t], xi + FIRST)
                        for j in range(NB):
                            for h in range(HALVES):
                                act.activation(spl[:, j, h, tok], xc[par][:, h, tok], ACT.Tanh,
                                               scale=hbase[:, h, j:j + 1])
                        act.activation(slu[:, :, tok], xc[par][:, :, tok], ACT.Tanh, scale=0.5)\
                            .then_inc(tanh_ready, 1)
                if back:
                    act.wait_ge(v_psum, n)
                    act.activation(vt[:].rearrange("p t n -> p (t n)"), p_v[:, 0:CH], ACT.Copy).then_inc(v_ready, 1)
                    act.wait_ge(kneg_ready, n)
                    act.activation(kcorr[:], kmax[:], ACT.Exp, bias=kneg[:, 0:1])
                    act.activation(ek[:], p_k[:, 0:CH], ACT.Exp, bias=kneg[:, 0:1], accum_out=zchunk[:, 0:1])\
                        .then_inc(ek_ready, 1)
                    act.wait_ge(qs_ready, n)
                    act.activation(qt[:], qt[:], ACT.Exp).then_inc(q_exp, 1)
                    act.wait_ge(e_psum, n)
                    act.activation(ekT[:].rearrange("p t n -> p (t n)"), p_e, ACT.Copy).then_inc(eT_ready, 1)
                if mid:
                    act.wait_ge(uT_psum, n + 1)
                    act.activation(unT[:].rearrange("p h n -> p (h n)"), p_uT[:, 0:HALVES * CH], ACT.Copy)\
                        .then_inc(uT_ready, 1)
                if back:
                    hold(act, qT_psum, n)
                    act.activation(slots(number(act, b, m - 1), b, 0), p_qT[:, 0:CH].rearrange("p (k s) -> p k s", s=U),
                                   ACT.Copy).then_inc(qT_ready, 1)

            def out_step(b, m, back, mid, front, ahead, par):
                n = act.snap(b * C + m)
                if front:
                    act.wait_ge(y_ready, n + 2 + FIRST)
                    for t in range(TPC):
                        ins = act.activation(squares[:, t, :], y_of[par][:, t, :], ACT.Square, accum_out=sumsq[:, t:t + 1])
                    ins.then_inc(sq_ready, 1)
                if back:
                    hold(act, b_uT, n + FIRST)
                    for h in range(HALVES):
                        ins = act.activation(slots(number(act, b, m - 1), b, h), p_uT[:, h * CH:(h + 1) * CH]
                                             .rearrange("p (k s) -> p k s", s=U), ACT.Copy)
                    ins.then_inc(xr_ready, 1)
                if ahead:
                    if not front:
                        hold(act, qT_ready, b * C + C)
                    if mid:
                        hold(act, y_psum, n + 1)
                    act.activation(qTt[1 - par].rearrange("p (k s) -> p k s", s=U),
                                   slots(number(act, b, m + 2), b, 0), ACT.Copy).then_inc(qT_back, 1)

            with act.Fori(0, B) as b:
                chunk_steps(act, b, step)
                act.wait_ge(cT_psum, b + 1)
                act.activation(cT[:], p_c[:, 0:P], ACT.Copy).then_inc(cT_ready, 1)
                act.wait_ge(cw_psum, b + 1)
                act.activation(cw[:], p_c[:, P:P + E], ACT.Copy).then_inc(cw_ready, 1)
                out_steps(act, b, out_step)

        @block.tensor
        def _(pe):
            pe.wait_ge(consts, 10 + HEADS)
            pe.wait_ge(prep, 5)
            for j in range(NB):
                for h in range(HALVES):
                    pe.matmul(p_tok[0][:, 0:E], ones[:], wsp[:, j, h, :], start=(j == 0 and h == 0), stop=False)
            for i in range(2):
                mm = pe.matmul(p_tok[0][:, 0:E], ones[0:1, :], bias_rows[0:1, i, :], start=False, stop=(i == 1))
            mm.then_inc(bias_psum, 1)
            pe.wait_ge(mem_exp, 1)
            pe.transpose(p_c[0:MEM, 0:P], mem_e[:], ident[:]).then_inc(mem_tr, 1)
            pe.wait_ge(mem_trs, 1)
            pe.matmul(p_c[:, P:2 * P], mem_eT[:], mv[:], start=True, stop=True).then_inc(mem_c, 1)
            pe.wait_ge(setup_done, 1)

            def tokens(b, m, t):
                xi = pe.snap(b * CI + m + 1)
                tok = slice(t * P, (t + 1) * P)
                pe.wait_ge(h_ready[t], xi + FIRST)
                pe.wait_ge(silu_ready, xi * TPC + (t + 1 + 2 * TPC))
                for j in range(NB):
                    for h in range(HALVES):
                        pe.matmul(p_tok[t][:, 0:E], spl[:, j, h, tok], wsp[:, j, h, :],
                                  start=(j == 0 and h == 0), stop=False)
                for h in range(HALVES):
                    mm = pe.matmul(p_tok[t][:, 0:E], slu[:, h, tok], wba[:, h, :], start=False, stop=(h == 1))
                mm.then_inc(tok_psum[t], 1)

            def turn_un(done):
                for h in range(HALVES):
                    for t in range(TPC):
                        mm = pe.transpose(p_uT[:, h * CH + t * P:h * CH + (t + 1) * P],
                                          un[:, t, h * P:(h + 1) * P], ident[:])
                mm.then_inc(done, 1)

            def step(b, m, back, mid, front, par):
                n = pe.snap(b * C + m)
                if front == "image":
                    tokens(b, m, 0)
                if back:
                    pe.wait_ge(c_done, n - 1 + FIRST)
                    pe.wait_ge(ek_ready, n)
                    for t in range(TPC):
                        mm = pe.transpose(p_e[:, t * P:(t + 1) * P], ek[:, t * P:(t + 1) * P], ident[:])
                    mm.then_inc(e_psum, 1)
                if mid:
                    pe.wait_ge(un_ready, n + 1 + FIRST)
                    turn_un(uT_psum)
                if back:
                    pe.wait_ge(qn_ready, n)
                    for t in range(TPC):
                        mm = pe.transpose(p_qT[:, t * P:(t + 1) * P], qt[:, t, :], ident[:])
                    mm.then_inc(qT_psum, 1)
                    pe.wait_ge(eT_ready, n)
                    for t in range(TPC):
                        mm = pe.matmul(p_c[:, 0:P], ekT[:, t, :], vt[:, t, :], start=(t == 0), stop=(t == TPC - 1))
                    mm.then_inc(c_psum, 1)
                if front == "image":
                    tokens(b, m, 1)
                if mid:
                    pe.wait_ge(uT_ready, n + 1)
                    for h in range(HALVES):
                        mm = pe.matmul(p_k[:, 0:CH], wqkv[:, h, P:2 * P], unT[:, h, :], start=(h == 0), stop=(h == 1))
                    mm.then_inc(k_psum, 1)
                    for part, bank, done in ((0, p_q, q_psum), (2, p_v, v_psum)):
                        for t in range(TPC):
                            for h in range(HALVES):
                                mm = pe.matmul(bank[:, t * P:(t + 1) * P], unT[:, h, t * P:(t + 1) * P],
                                               wqkv[:, h, part * P:(part + 1) * P], start=(h == 0), stop=(h == 1))
                        mm.then_inc(done, 1)

            def out_step(b, m, back, mid, front, ahead, par):
                n = pe.snap(b * C + m)
                if front:
                    if mid:
                        hold(pe, y_ready, n + FIRST)
                    hold(pe, qT_back, n + 2)
                    for t in range(TPC):
                        mm = pe.matmul(p_tok[par][:, t * E:(t + 1) * E],
                                       qTt[par][:, t * P:(t + 1) * P], cw[:], start=True, stop=True)
                    mm.then_inc(y_psum, 1)
                if back:
                    pe.wait_ge(b_un, n + FIRST)
                    pe.wait_ge(xr_ready, n - 1 + FIRST)
                    turn_un(b_uT)

            with pe.Fori(0, B) as b:
                chunk_steps(pe, b, step)
                pe.wait_ge(cn_ready, b + 1)
                pe.transpose(p_c[:, 0:P], cnorm[:], ident[:]).then_inc(cT_psum, 1)
                pe.wait_ge(cT_ready, b + 1)
                pe.matmul(p_c[:, P:P + E], cT[:], wo[:], start=True, stop=True).then_inc(cw_psum, 1)
                hold(pe, cw_ready, b + 1)
                out_steps(pe, b, out_step)

        @block.vector
        def _(dve):
            dve.wait_ge(weights_in, 16 * 12)
            dve.tensor_scalar(hbase[:], hbase[:], 0.5, None, ALU.mult).then_inc(prep, 1)
            dve.tensor_scalar(wsp[:].rearrange("p j h e -> p (j h e)"), wsp[:].rearrange("p j h e -> p (j h e)"),
                              0.5, None, ALU.mult).then_inc(prep, 1)
            dve.tensor_scalar(wba[:], wba[:], 0.5, None, ALU.mult).then_inc(prep, 1)
            for h in range(HALVES):
                ins = dve.tensor_scalar(wqkv[:, h, :], wqkv[:, h, :], gpre[:, h:h + 1], None, ALU.mult)
            ins.then_inc(prep, 1)
            dve.tensor_reduce(mem_max[:], mk[:], AX.X, ALU.max).then_inc(prep, 1)
            dve.wait_ge(prep, 5)
            dve.tensor_scalar(mem_neg[:], mem_max[:], -1.0, None, ALU.mult).then_inc(prep, 1)
            dve.tensor_scalar(go[:], go[:], ROOT_E, None, ALU.mult)
            dve.wait_ge(bias_psum, 1)
            dve.tensor_copy(tok_bias[:], p_tok[0][:, 0:E]).then_inc(prep, 1)
            dve.wait_ge(mem_tr, 1)
            dve.tensor_copy(mem_eT[:], p_c[0:MEM, 0:P]).then_inc(mem_trs, 1)
            dve.wait_ge(mem_c, 1)
            dve.tensor_copy(mem_ctx[:], p_c[:, P:2 * P]).then_inc(setup_done, 1)
            dve.sem_inc(silu_ready, 2 * TPC)
            dve.wait_ge(setup_done, 1)
            dve.wait_ge(consts, 10 + HEADS)

            def tile_stats(src, k):
                for t in range(TPC):
                    dve.bn_stats(stats[:, t, :], src[:, t, :]).then_inc(stat_a, 1)
                hold(dve, stat_a, k * TPC + TPC)
                for t in range(TPC):
                    dve.bn_aggr(mvar[:, t, :], stats[:, t, :]).then_inc(stat_b, 1)
                dve.wait_ge(stat_b, k * TPC + TPC)
                dve.tensor_tensor(vroot[:], mvar[:, :, 1].unsqueeze(1).broadcast_to([P, 2, TPC]), eps2[:],
                                  ALU.add).then_inc(roots_in, 1)

            def new_state(b):
                for q in range(2):
                    hold(dve, h1_stored[q], b * (8 * C) + FIRST)
                dve.tensor_copy(kmax[:], mem_max[:]).then_inc(state0, 1)
                dve.tensor_copy(zsum[:], mem_z[:]).then_inc(state0, 1)
                dve.tensor_copy(cacc[:], mem_ctx[:]).then_inc(state0, 1)
                hold(dve, state0, b * 4 + 3)

            def silu(b, m, t, par):
                tok = slice(t * P, (t + 1) * P)
                dve.wait_ge(tanh_ready, (b * CI + m) * TPC + (t + 1 + TPC))
                dve.scalar_tensor_tensor(slu[:, :, tok], slu[:, :, tok], 1.0, xc[par][:, :, tok], ALU.add, ALU.mult)\
                    .then_inc(silu_ready, 1)

            def take_h(b, m, t):
                n = dve.snap(b * C + m)
                hold(dve, s_ready, n * TPC + FIRST)
                hold(dve, un_ready, n + FIRST)
                dve.wait_ge(tok_psum[t], b * CI + m + 1 + FIRST)
                dve.tensor_tensor(ht[:, t, :], p_tok[t][:, 0:E], tok_bias[:], ALU.add).then_inc(h_ready[t], 1)

            q3 = p_q[:, 0:CH].rearrange("p (g d) -> p g d", d=DH)
            qt3 = qt[:].rearrange("p t (g d) -> p (t g) d", d=DH)
            G = TPC * HEADS

            def step(b, m, back, mid, front, par, image=True):
                n = dve.snap(b * C + m)
                if front == "image":
                    silu(b, m, 0, par)
                if mid:
                    k = dve.snap(b * (2 * C) + m)
                    if image:
                        take_h(b, m, 1)
                        hold(dve, h_ready[0], b * CI + m + 1 + FIRST)
                        hold(dve, h_ready[1], b * CI + m + 1 + FIRST)
                    else:
                        hold(dve, txt_in, b * (16 * CT) + (m - CI) * 16 + 16)
                    tile_stats(ht, k)
                if back:
                    dve.wait_ge(k_psum, n)
                    k2 = dve.snap(n * 2 - 2)
                    dve.tensor_reduce(kchunk[:], p_k[:, 0:CH], AX.X, ALU.max).then_inc(kstep, 1)
                    dve.wait_ge(kstep, k2 + 1)
                    dve.tensor_tensor(knew[:], kmax[:], kchunk[:], ALU.max).then_inc(kstep, 1)
                    dve.wait_ge(kstep, k2 + 2)
                    dve.tensor_scalar(kneg[:], knew[:], -1.0, None, ALU.mult).then_inc(kneg_ready, 1)
                    dve.wait_ge(q_psum, n)
                    q3n = dve.snap(n * 3 - 3)
                    dve.tensor_reduce(qmax[:], q3, AX.X, ALU.max).then_inc(qstep, 1)
                    dve.wait_ge(qstep, q3n + 1)
                    dve.tensor_tensor(qt3, q3, qmax[:].unsqueeze(2).broadcast_to([P, G, DH]), ALU.subtract)\
                        .then_inc(qs_ready, 1)
                if mid:
                    dve.wait_ge(roots, k + 1)
                    s6 = dve.snap(n * 6)
                    dve.tensor_tensor(nrm[:], proot[:, 0, :], proot[:, 1, :], ALU.mult).then_inc(small, 1)
                    dve.tensor_scalar(sone[:], proot[:, 0, :], 1.0, None, ALU.add).then_inc(small, 1)
                    dve.wait_ge(small, s6 + 2)
                    dve.tensor_scalar(nrm[:], nrm[:], NORM_MIN / ROOT_E, None, ALU.max).then_inc(small, 1)
                    dve.scalar_tensor_tensor(smean[:], mvar[:, :, 0], -1.0, proot[:, 0, :], ALU.mult, ALU.mult)\
                        .then_inc(small, 1)
                    dve.wait_ge(small, s6 + 4)
                    dve.reciprocal(rnrm[:], nrm[:]).then_inc(small, 1)
                    dve.wait_ge(small, s6 + 5)
                    dve.tensor_tensor(scl[:], rnrm[:], proot[:, 0, :], ALU.mult).then_inc(small, 1)
                    dve.wait_ge(small, s6 + 6)
                    for t in range(TPC):
                        ins = dve.tensor_scalar(un[:, t, :], ht[:, t, :], mvar[:, t, 0:1], scl[:, t:t + 1],
                                                ALU.subtract, ALU.mult)
                    ins.then_inc(un_ready, 1)
                if back:
                    dve.wait_ge(q_exp, n)
                    dve.tensor_reduce(qsum[:], qt3, AX.X, ALU.add).then_inc(qstep, 1)
                    dve.wait_ge(qstep, q3n + 2)
                    dve.reciprocal(qsum[:], qsum[:]).then_inc(qstep, 1)
                    dve.wait_ge(qstep, q3n + 3)
                    dve.tensor_tensor(qt3, qt3, qsum[:].unsqueeze(2).broadcast_to([P, G, DH]), ALU.mult)\
                        .then_inc(qn_ready, 1)
                    dve.wait_ge(ek_ready, n)
                    dve.tensor_copy(kmax[:], knew[:])
                    dve.scalar_tensor_tensor(zsum[:], zsum[:], kcorr[:, 0:1], zchunk[:], ALU.mult, ALU.add)
                if front == "image":
                    silu(b, m, 1, par)
                    take_h(b, number(dve, b, m + 1), 0)
                if back:
                    dve.wait_ge(c_psum, n)
                    dve.scalar_tensor_tensor(cacc[:], cacc[:], kcorr[:, 0:1], p_c[:, 0:P], ALU.mult, ALU.add)\
                        .then_inc(c_done, 1)
                    hold(dve, c_done, n + FIRST)

            def out_step(b, m, back, mid, front, ahead, par):
                n = dve.snap(b * C + m)
                y = y_of[par]
                if front:
                    dve.wait_ge(y_psum, n + 2)
                    dve.tensor_tensor(y[:], p_tok[par][:].rearrange("p (t e) -> p t e", e=E),
                                      bo[:].unsqueeze(1).broadcast_to([P, TPC, E]), ALU.add).then_inc(y_ready, 1)
                if mid:
                    k = dve.snap(b * (2 * C) + C + m)
                    h1 = h1_of[1 - par]
                    dve.wait_ge(h1_ready, n + 1 + FIRST)
                    tile_stats(h1, k)
                if front:
                    dve.wait_ge(ynorm, n + 2)
                    dve.tensor_scalar(nrm[:], nrm[:], NORM_MIN, None, ALU.max).then_inc(ysm, 1)
                    dve.wait_ge(ysm, n * 2 + 3)
                    dve.reciprocal(rnrm[:], nrm[:]).then_inc(ysm, 1)
                    dve.wait_ge(ysm, n * 2 + 4)
                    for t in range(TPC):
                        ins = dve.scalar_tensor_tensor(y[:, t, :], y[:, t, :], rnrm[:, t:t + 1], go[:],
                                                       ALU.mult, ALU.mult)
                    ins.then_inc(yg_ready, 1)
                if mid:
                    hold(dve, b_uT, n + FIRST)
                    dve.wait_ge(roots, k + 1)
                    for t in range(TPC):
                        ins = dve.tensor_scalar(un[:, t, :], h1[:, t, :], mvar[:, t, 0:1], proot[:, 0, t:t + 1],
                                                ALU.subtract, ALU.mult)
                    ins.then_inc(b_un, 1)

            def chunk_step(b, m, back, mid, front, par):
                step(b, m, back, mid, front, par, image=back is False or not isinstance(m, int) or m < CI)

            with dve.Fori(0, B) as b:
                new_state(b)
                chunk_steps(dve, b, chunk_step)
                dve.reciprocal(zinv[:], zsum[:]).then_inc(state0, 1)
                dve.wait_ge(state0, b * 4 + 4)
                dve.scalar_tensor_tensor(cnorm[:], cacc[:], zinv[:, 0:1], head_mask[:], ALU.mult, ALU.mult)\
                    .then_inc(cn_ready, 1)
                out_steps(dve, b, out_step)


GATES = (2, 0, 1, 3)


def scan_phase(nc, ctx_outer, xr, ident, ones, inc_tot, args):
    w_hh, w_ih, b_ih, b_hh, w_lin, b_lin, fw, bw, h_dram, n_blocks, B = args
    COLS = B * U
    assert n_blocks % 2 == 0 and COLS == P
    G2 = 2

    with ExitStack() as ctx:
        def sb(name, shape, dt=F32):
            return ctx.enter_context(nc.sbuf_tensor(name, shape, dt))

        def sem(name):
            return ctx.enter_context(nc.semaphore(name))

        w1 = sb("w1", [P, HALVES, 8, P], F16)
        w2 = sb("w2", [P, HALVES, 8, P], F16)
        wih = sb("wih", [P, HALVES, 8, P])
        wst = wih
        brow = sb("brow", [1, 2, 8 * P])
        bsum = sb("bsum", [1, 8 * P])
        bpart = sb("bpart", [1, 3, 8 * P], F16)
        bias3 = sb("bias3", [3, 8 * P], F16)
        ones3 = sb("ones3", [3, COLS], F16)
        wlin = sb("wlin", [P, HALVES, 2])
        wdiff = sb("wdiff", [P, HALVES, P])
        wd1 = sb("wd1", [P, HALVES])
        blin = sb("blin", [P, 2])
        bdiff = sb("bdiff", [P, 1])
        fwt = sb("fwt", [P, HALVES])
        bwt = sb("bwt", [P, HALVES])
        nfw = sb("nfw", [P, HALVES])
        fmb = sb("fmb", [P, HALVES])
        hop = sb("hop", [P, 2, 2, HALVES, B], F16)
        gi = sb("gi", [P, HALVES, 2 * B])
        fo = sb("fo", [P, HALVES, 2, B, 2])
        cpair = sb("cpair", [P, HALVES, 2, 2 * B + 2])
        tc = sb("tc", [P, HALVES, B])
        hblk = [sb(f"hblk{i}", [P, HALVES, B, U]) for i in range(2)]
        mask = sb("mask", [P, COLS])
        wm = sb("wm", [P, HALVES, COLS])
        part = sb("part", [P, HALVES, COLS])
        inc = [sb(f"inc{i}", [P, HALVES, COLS]) for i in range(2)]
        inct = sb("inct", [P, HALVES, COLS])
        keep = sb("keep", [P, COLS])
        hres = sb("hres", [P, E])
        first_sig = sb("first_sig", [P, 1])

        gp = [[[ctx.enter_context(nc.psum_tensor(f"g{s}{h}{q}", [P, 512], F32)) for q in range(2)]
               for h in range(HALVES)] for s in range(2)]

        def gates(s, half, pair):
            return gp[s][half][pair][:, 0:G2 * COLS].rearrange("p (g b t) -> p g b t", g=G2, b=B)

        hold = holder(sem("held2"))
        lw = sem("lw")
        lw2 = sem("lw2")
        lw3 = sem("lw3")
        pre = sem("pre")
        pset = sem("pset")
        z0 = sem("z0")
        gi_psum = [sem("gi_psum0"), sem("gi_psum1")]
        fo_psum = [sem("fo_psum0"), sem("fo_psum1")]
        i_ready = [sem("i_ready0"), sem("i_ready1")]
        cin = [sem("cin0"), sem("cin1")]
        c_new = [sem("c_new0"), sem("c_new1")]
        tc_ready = [sem("tc_ready0"), sem("tc_ready1")]
        h1_out = [sem("h1_out0"), sem("h1_out1")]
        h_out = [sem("h_out0"), sem("h_out1")]
        h2_out = [sem("h2_out0"), sem("h2_out1")]
        x_psum = sem("x_psum")
        logit_psum = sem("logit_psum")
        mask_ready = sem("mask_ready")
        pstep = sem("pstep")
        wm_ready = sem("wm_ready")
        inc_ready = sem("inc_ready")
        part_ready = sem("part_ready")
        part_psum = sem("part_psum")
        res_in = sem("res_in")
        out_ready = sem("out_ready")
        PSTEPS = 7

        block = ctx.enter_context(nc.Block())

        @block.sync
        def _(sp):
            sp.dma_start(wst[:], w_hh).then_inc(lw, 16)
            sp.dma_start(brow[0:1, 0, :], b_ih).then_inc(lw2, 16)
            sp.dma_start(brow[0:1, 1, :], b_hh).then_inc(lw2, 16)
            sp.dma_start(wlin[:], w_lin).then_inc(lw2, 16)
            sp.dma_start(blin[:], b_lin.broadcast_to([P, 2])).then_inc(lw2, 16)
            sp.dma_start(fwt[:], fw).then_inc(lw2, 16)
            sp.dma_start(bwt[:], bw).then_inc(lw2, 16)
            sp.wait_ge(pre, 4)
            sp.dma_start(wih[:], w_ih).then_inc(lw3, 16)
            sp.wait_ge(pset, 3)
            for r in range(3):
                sp.dma_start(bias3[r:r + 1, :], bpart[0:1, r, :]).then_inc(lw3, 16)

            def residual(j):
                hold(sp, out_ready, j + FIRST)
                sp.dma_start(hres[:], h_dram[:, bass.ds(j * U, U), :]).then_inc(res_in, 16)

            with sp.Fori(0, n_blocks // 2) as i:
                for s in range(2):
                    residual(sp.snap(i * 2 + s))
            residual(n_blocks)
            sp.wait_ge(res_in, 16 * (n_blocks + 1))

        @block.gpsimd
        def _(pool):
            for start in (out_ready, inc_ready, *h1_out, *h2_out):
                pool.sem_inc(start, FIRST)
            for t in (hop, cpair, fo, hblk[1], inc[0], inc[1]):
                pool.memset(t[:], 0.0).then_inc(z0, 1)
            pool.memset(ones3[:], H_SCALE).then_inc(z0, 1)
            pool.memset(keep[:], 1.0).then_inc(z0, 1)
            pool.wait_ge(z0, 8)
            pool.memset(keep[:].rearrange("p (b t) -> p b t", b=B)[:, :, 0], 0.0).then_inc(z0, 1)
            pool.wait_ge(z0, 9)
            pool.wait_ge(pre, 10)

            def post(j, s):
                h = hblk[1 - s]
                hv = h[:].rearrange("p h b t -> p h (b t)")
                j7 = pool.snap(j * PSTEPS)
                pool.wait_ge(mask_ready, j + 1)
                pool.tensor_tensor(wm[:], hv, mask[:].unsqueeze(1).broadcast_to([P, HALVES, COLS]), ALU.mult)\
                    .then_inc(pstep, 1)
                for k in range(HALVES):
                    hold(pool, pstep, j7 + 1 + k)
                    pool.tensor_scalar(part[:, k, :], mask[:], nfw[:, k:k + 1], 2.0, ALU.mult, ALU.add)\
                        .then_inc(pstep, 1)
                pool.wait_ge(pstep, j7 + 3)
                pool.tensor_tensor(part[:], part[:], hv, ALU.mult).then_inc(pstep, 1)
                first = wm[:].rearrange("p h (b t) -> p h b t", b=B)[:, :, :, 0]
                last = inc[s][:].rearrange("p h (b t) -> p h b t", b=B)[:, :, :, U - 1]
                pool.wait_ge(inc_ready, j * HALVES + FIRST)
                pool.tensor_tensor(first, first, last, ALU.add).then_inc(wm_ready, 1)
                hold(pool, inc_ready, j * HALVES + HALVES + FIRST)
                for k in range(HALVES):
                    pool.tensor_scalar(inct[:, k, :], inc[1 - s][:, k, :], fmb[:, k:k + 1], None, ALU.mult)\
                        .then_inc(pstep, 1)
                pool.wait_ge(pstep, j7 + 6)
                pool.tensor_tensor(part[:], part[:], inct[:], ALU.add).then_inc(part_ready, 1)
                pool.wait_ge(part_ready, j + 1)
                pool.sem_inc(pstep, 1)

            with pool.Fori(0, n_blocks // 2) as i:
                for s in range(2):
                    post(pool.snap(i * 2 + s), s)
            post(n_blocks, 0)

        @block.scalar
        def _(act):
            act.wait_ge(z0, 9)
            act.activation(first_sig[:], keep[:, 0:1], ACT.Sigmoid)
            with act.Fori(0, n_blocks // 2) as i:
                base = act.snap(i * (2 * U))
                for s in range(2):
                    for t in range(U):
                        step = s * U + t
                        nxt = 1 - step % 2

                        def gate_gi(h):
                            act.wait_ge(gi_psum[h], base + step + 1)
                            act.activation(gi[:, h, :].rearrange("p (g b) -> p g b", g=G2), gates(s, h, 0)[:, :, :, t],
                                           ACT.Tanh, scale=1.0 / GATE_SCALE).then_inc(i_ready[h], 1)

                        def gate_fo(h):
                            act.wait_ge(fo_psum[h], base + step + 1)
                            act.activation(fo[:, h, :, :, 1], gates(s, h, 1)[:, :, :, t], ACT.Sigmoid,
                                           scale=1.0 / GATE_SCALE).then_inc(cin[h], 1)

                        def tanh_c(h):
                            act.wait_ge(c_new[h], base + step + 1)
                            act.activation(tc[:, h, :], cpair[:, h, nxt, 1:2 * B:2], ACT.Tanh, scale=0.5)\
                                .then_inc(tc_ready[h], 1)

                        gate_gi(0)
                        gate_fo(0)
                        gate_gi(1)
                        gate_fo(1)
                        tanh_c(0)
                        tanh_c(1)

        @block.tensor
        def _(pe):
            pe.wait_ge(z0, 9)
            pe.wait_ge(pre, 10)
            pe.wait_ge(lw3, 64)

            def x_bias(s, half, pair, g):
                m = half * 4 + pair * 2 + g
                pe.matmul(gates(s, half, pair)[:, g, :, :].rearrange("p b t -> p (b t)"),
                          bias3[:, m * P:(m + 1) * P], ones3[:], start=(g == 0), stop=False, skip_group_check=True)

            def x_part(s, half, pair, g, kc, j):
                m = half * 4 + pair * 2 + g
                return pe.matmul(gates(s, half, pair)[:, g, :, :].rearrange("p b t -> p (b t)"), wih[:, kc, m, :],
                                 xr[:, bass.ds(j + 1, 1), kc, :, :].rearrange("p k b t -> p (k b t)"),
                                 start=False, stop=False, skip_group_check=True)

            slots = [(half, pair, g, kc) for half in range(HALVES) for pair in range(2) for g in range(2)
                     for kc in range(HALVES)]

            def logits(s, kc):
                mm = pe.matmul(gp[1 - s][0][0][:, G2 * COLS:G2 * COLS + COLS], wdiff[:, kc, :],
                               hblk[1 - s][:, kc, :, :].rearrange("p b t -> p (b t)"),
                               start=(kc == 0), stop=(kc == HALVES - 1), skip_group_check=True)
                if kc == HALVES - 1:
                    mm.then_inc(logit_psum, 1)

            def turn(s, j):
                pe.wait_ge(part_ready, j + 1)
                for k in range(HALVES):
                    mm = pe.transpose(gp[1 - s][0][1][:, G2 * COLS + k * P:G2 * COLS + (k + 1) * P],
                                      part[:, k, :], ident[:])
                mm.then_inc(part_psum, 1)

            for half, pair, g, kc in slots:
                if kc == 0:
                    x_bias(0, half, pair, g)
                x_part(0, half, pair, g, kc, 0)

            PASSES = ((w2, 0, h1_out), (w1, 0, h1_out), (w1, 1, h2_out))
            EARLY = ((0, 0), (0, 1), (0, 2), (0, 3), (1, 0), (1, 1), (1, 2))

            with pe.Fori(0, n_blocks // 2) as i:
                base = pe.snap(i * (2 * U))
                for s in range(2):
                    j = pe.snap(i * 2 + s)
                    for t in range(U):
                        step = s * U + t
                        par = step % 2

                        def mm(wt, hp, kc, half, m):
                            return pe.matmul(gates(s, half, m // 2)[:, m % 2, :, t], wt[:, kc, half * 4 + m, :],
                                             hop[:, par, hp, kc, :], start=False, stop=False,
                                             skip_group_check=True)

                        for wt, hp, ready in PASSES:
                            if wt is not w1 or hp:
                                pe.wait_ge(ready[0], base + (step + FIRST))
                            for half, m in EARLY:
                                mm(wt, hp, 0, half, m)
                        for wt, hp, ready in PASSES:
                            if wt is not w1 or hp:
                                pe.wait_ge(ready[1], base + (step + FIRST))
                            for m in range(2):
                                last = mm(wt, hp, 1, 0, m)
                        last.then_inc(gi_psum[0], 1)
                        for wt, hp, _ in PASSES:
                            for m in range(2, 4):
                                last = mm(wt, hp, 1, 0, m)
                        last.then_inc(fo_psum[0], 1)
                        for wt, hp, _ in PASSES:
                            for m in range(2):
                                last = mm(wt, hp, 1, 1, m)
                        last.then_inc(gi_psum[1], 1)
                        for wt, hp, _ in PASSES:
                            for m in (3,):
                                mm(wt, hp, 0, 1, m)
                        for wt, hp, _ in PASSES:
                            for m in range(2, 4):
                                last = mm(wt, hp, 1, 1, m)
                        last.then_inc(fo_psum[1], 1)
                        if t < HALVES:
                            logits(s, t)
                        if t == 12:
                            turn(s, j)
                        if t == 15:
                            pe.wait_ge(out_ready, j + 1 + FIRST)
                        if 15 <= t < 15 + len(slots):
                            half, pair, g, kc = slots[t - 15]
                            if kc == 0:
                                x_bias(1 - s, half, pair, g)
                            x_part(1 - s, half, pair, g, kc, j + 1)
            for h in range(HALVES):
                pe.wait_ge(h2_out[h], n_blocks * U + FIRST)
            logits(0, 0)
            logits(0, 1)
            turn(0, n_blocks)

        @block.vector
        def _(dve):
            flat = "p h m c -> p (h m c)"
            dve.wait_ge(lw, 16)
            halved = sem("halved")
            for k in range(HALVES):
                dve.tensor_scalar(wst[:, k, 1::4, :], wst[:, k, 1::4, :], 0.5, None, ALU.mult).then_inc(halved, 1)
            dve.wait_ge(halved, HALVES)
            dve.tensor_scalar(wst[:].rearrange(flat), wst[:].rearrange(flat), W_SCALE, None, ALU.mult).then_inc(pre, 1)
            dve.wait_ge(pre, 1)
            dve.tensor_copy(w1[:].rearrange(flat), wst[:].rearrange(flat)).then_inc(pre, 1)
            dve.wait_ge(pre, 2)
            dve.tensor_tensor(w2[:].rearrange(flat), wst[:].rearrange(flat), w1[:].rearrange(flat), ALU.subtract)\
                .then_inc(pre, 1)
            dve.wait_ge(pre, 3)
            dve.sem_inc(pre, 1)
            dve.wait_ge(lw2, 96)
            dve.tensor_tensor(bsum[:], brow[0:1, 0, :], brow[0:1, 1, :], ALU.add).then_inc(pset, 1)
            dve.wait_ge(pset, 1)
            i_bias = bsum[:].rearrange("o (m c) -> o m c", c=P)[:, 1::4, :]
            dve.tensor_scalar(i_bias, i_bias, 0.5, None, ALU.mult).then_inc(halved, 1)
            dve.wait_ge(halved, HALVES + 1)
            dve.tensor_scalar(bsum[:], bsum[:], W_SCALE, None, ALU.mult).then_inc(pset, 1)
            dve.wait_ge(pset, 2)
            bs = sem("bs")
            dve.tensor_copy(bpart[0:1, 0, :], bsum[:]).then_inc(bs, 1)
            dve.wait_ge(bs, 1)
            dve.tensor_tensor(bsum[:], bsum[:], bpart[0:1, 0, :], ALU.subtract).then_inc(bs, 1)
            dve.wait_ge(bs, 2)
            dve.tensor_copy(bpart[0:1, 1, :], bsum[:]).then_inc(bs, 1)
            dve.wait_ge(bs, 3)
            dve.tensor_tensor(bsum[:], bsum[:], bpart[0:1, 1, :], ALU.subtract).then_inc(bs, 1)
            dve.wait_ge(bs, 4)
            dve.tensor_copy(bpart[0:1, 2, :], bsum[:]).then_inc(pset, 1)
            dve.tensor_tensor(wd1[:], wlin[:, :, 1], wlin[:, :, 0], ALU.subtract).then_inc(pre, 1)
            dve.wait_ge(pre, 5)
            dve.tensor_copy(wdiff[:], wd1[:].unsqueeze(2).broadcast_to([P, HALVES, P])).then_inc(pre, 1)
            dve.tensor_tensor(bdiff[:], blin[:, 1:2], blin[:, 0:1], ALU.subtract).then_inc(pre, 1)
            dve.tensor_scalar(nfw[:], fwt[:], -1.0, None, ALU.mult).then_inc(pre, 1)
            dve.tensor_tensor(fmb[:], fwt[:], bwt[:], ALU.subtract).then_inc(pre, 1)
            dve.wait_ge(lw3, 64)
            for k in range(HALVES):
                dve.tensor_scalar(wih[:, k, 1::4, :], wih[:, k, 1::4, :], 0.5, None, ALU.mult).then_inc(halved, 1)
            dve.wait_ge(halved, 2 * HALVES + 1)
            dve.tensor_scalar(wih[:].rearrange(flat), wih[:].rearrange(flat), GATE_SCALE, None, ALU.mult).then_inc(pre, 1)
            dve.wait_ge(z0, 9)
            dve.wait_ge(pre, 10)

            def to_mask(s, j):
                dve.wait_ge(logit_psum, j + 1)
                dve.tensor_scalar(mask[:], gp[1 - s][0][0][:, G2 * COLS:G2 * COLS + COLS], bdiff[:, 0:1], 0.0,
                                  ALU.add, ALU.is_gt).then_inc(mask_ready, 1)

            def run_sum(s, j, k):
                dve.wait_ge(wm_ready, j + 1)
                dve.tensor_tensor_scan(inc[1 - s][:, k, :], keep[:], wm[:, k, :], 0.0, ALU.mult, ALU.add)\
                    .then_inc(inc_ready, 1)

            def add_residual(s, j):
                dve.wait_ge(res_in, j * 16 + 16)
                dve.wait_ge(part_psum, j + 1)
                dve.tensor_tensor(xr[:, bass.ds(j, 1), :, :, :].rearrange("p k h b t -> p (k h b t)"),
                                  gp[1 - s][0][1][:, G2 * COLS:G2 * COLS + E], hres[:], ALU.add)\
                    .then_inc(out_ready, 1)

            with dve.Fori(0, n_blocks // 2) as i:
                base = dve.snap(i * (2 * U))
                base2 = dve.snap(i * (4 * U))
                for s in range(2):
                    j = dve.snap(i * 2 + s)
                    for t in range(U):
                        step = s * U + t
                        par, nxt = step % 2, 1 - step % 2

                        def i_times_g(h):
                            dve.wait_ge(i_ready[h], base + step + 1)
                            dve.scalar_tensor_tensor(cpair[:, h, par, 2:2 * B + 2:2], gi[:, h, B:2 * B], 1.0,
                                                     gi[:, h, 0:B], ALU.add, ALU.mult).then_inc(cin[h], 1)

                        def new_c(h):
                            dve.wait_ge(cin[h], base2 + 2 * step + 2)
                            dve.tensor_tensor_scan(cpair[:, h, nxt, 0:2 * B],
                                                   fo[:, h, 0, :, :].rearrange("p b two -> p (b two)"),
                                                   cpair[:, h, par, 1:2 * B + 1], 0.0, ALU.mult, ALU.add)\
                                .then_inc(c_new[h], 1)

                        def new_h(h):
                            o = fo[:, h, 1, :, 1]
                            dve.wait_ge(tc_ready[h], base + step + 1)
                            dve.scalar_tensor_tensor(hop[:, nxt, 0, h, :], o, H_SCALE, tc[:, h, :], ALU.mult, ALU.mult)\
                                .then_inc(h1_out[h], 1)
                            dve.tensor_tensor(hblk[s][:, h, :, t], o, tc[:, h, :], ALU.mult).then_inc(h_out[h], 1)

                        def rest_h(h):
                            dve.wait_ge(h_out[h], base + step + 1)
                            dve.scalar_tensor_tensor(hop[:, nxt, 1, h, :], hblk[s][:, h, :, t], H_SCALE,
                                                     hop[:, nxt, 0, h, :], ALU.mult, ALU.subtract)\
                                .then_inc(h2_out[h], 1)

                        i_times_g(0)
                        new_c(0)
                        i_times_g(1)
                        new_c(1)
                        new_h(0)
                        rest_h(0)
                        new_h(1)
                        rest_h(1)
                        if t == 2:
                            to_mask(s, j)
                        if t in (7, 8):
                            run_sum(s, j, t - 7)
                        if t == 14:
                            add_residual(s, j)
            to_mask(0, n_blocks)
            run_sum(0, n_blocks, 0)
            run_sum(0, n_blocks, 1)
            add_residual(0, n_blocks)
            dve.wait_ge(inc_ready, (n_blocks + 1) * HALVES + FIRST)
            total = inc[1][:].rearrange("p h (b t) -> p h b t", b=B)[:, :, :, U - 1:U]
            for k in range(HALVES):
                dve.tensor_scalar(inc_tot[:, k, :].rearrange("p (b t) -> p b t", b=B),
                                  total[:, k, :, :].broadcast_to([P, B, U]), bwt[:, k:k + 1], None, ALU.mult)


def suffix_phase(nc, xr, ident, inc_tot, out, n_blocks, B):
    K = 8
    assert n_blocks % K == 0
    with ExitStack() as ctx:
        tot = ctx.enter_context(nc.sbuf_tensor("tot", [P, E], F32))
        ps = ctx.enter_context(nc.psum_tensor("ps", [P, 512], F32))
        tot_psum = ctx.enter_context(nc.semaphore("tot_psum"))
        tot_ready = ctx.enter_context(nc.semaphore("tot_ready"))
        done = ctx.enter_context(nc.semaphore("done"))
        stored = ctx.enter_context(nc.semaphore("stored"))
        N = n_blocks // K
        block = ctx.enter_context(nc.Block())

        @block.tensor
        def _(pe):
            for k in range(HALVES):
                mm = pe.transpose(ps[:, k * P:(k + 1) * P], inc_tot[:, k, :], ident[:])
            mm.then_inc(tot_psum, 1)

        @block.vector
        def _(dve):
            dve.wait_ge(tot_psum, 1)
            dve.tensor_copy(tot[:], ps[:, 0:E]).then_inc(tot_ready, 1)
            dve.wait_ge(tot_ready, 1)
            with dve.Fori(0, N) as i:
                blk = xr[:, bass.ds(i * K + 1, K), :, :, :].rearrange("p k h b t -> p k (h b t)")
                dve.tensor_tensor(blk, blk, tot[:].unsqueeze(1).broadcast_to([P, K, E]), ALU.add).then_inc(done, 1)

        @block.sync
        def _(sp):
            with sp.Fori(0, N) as i:
                sp.wait_ge(done, i + 1)
                for b in range(B):
                    sp.dma_start(out[b, bass.ds(i * (K * U), K * U), :].rearrange("(k t) d -> t k d", t=U),
                                 xr[b * U:(b + 1) * U, bass.ds(i * K + 1, K), :, :, :]
                                 .rearrange("p k h b t -> p k (h b t)")).then_inc(stored, 16)
            sp.wait_ge(stored, 16 * B * N)


def build(nc, x, txt, bases, w_spline, b_spline, w_base, b_base, w_qkv, mem_k, mem_v, w_out, b_out, g_out, g_pre,
          w_ih, w_hh, b_ih, b_hh, w_lin, b_lin, fw, bw, out):
    B = x.shape[0]
    T = x.shape[2] + txt.shape[1]
    n_blocks = T // U
    s_dram = nc.dram_tensor("s_rows", (B, T, E), F32, kind="Internal").ap()
    h_dram = nc.dram_tensor("h_rows", (B, U + T, E), F32, kind="Internal").ap()
    with ExitStack() as ctx:
        xr = ctx.enter_context(nc.sbuf_tensor("xr", [P, n_blocks + 2, HALVES, B, U], F32))
        ident = ctx.enter_context(nc.sbuf_tensor("ident", [P, P], F32))
        ones = ctx.enter_context(nc.sbuf_tensor("ones", [P, P], F32))
        inc_tot = ctx.enter_context(nc.sbuf_tensor("inc_tot", [P, HALVES, B * U], F32))
        token_phases(nc, ctx, xr, ident, ones,
                     (x, txt, bases, w_spline, b_spline, w_base, b_base, w_qkv, mem_k, mem_v, w_out, b_out, g_out,
                      g_pre, s_dram, h_dram))
        scan_phase(nc, ctx, xr, ident, ones, inc_tot,
                   (w_hh, w_ih, b_ih, b_hh, w_lin, b_lin, fw, bw, h_dram, n_blocks, B))
        suffix_phase(nc, xr, ident, inc_tot, out, n_blocks, B)


def layout(inputs):
    import numpy as np
    a = {k: np.asarray(v) for k, v in inputs.items()}
    x = a["x"]
    B, C = x.shape[0], x.shape[1]

    def rows(w):
        return np.ascontiguousarray(w.reshape(HALVES, P, -1).transpose(1, 0, 2))

    def gate_tiles(w):
        v = w.reshape(4, HALVES, P, HALVES, P)[list(GATES)]
        return np.ascontiguousarray(v.transpose(4, 3, 1, 0, 2).reshape(P, HALVES, 8, P))

    def gate_row(b):
        return np.ascontiguousarray(b.reshape(4, HALVES, P)[list(GATES)].transpose(1, 0, 2).reshape(1, 8 * P))

    return {
        "x": np.ascontiguousarray(x.reshape(B, C, -1)),
        "txt": np.ascontiguousarray(a["txt"]),
        "bases": rows(a["L0_tok_bases"]),
        "w_spline": np.ascontiguousarray(a["L0_tok_W_spline"].T.reshape(HALVES, P, NB, E).transpose(1, 2, 0, 3)),
        "b_spline": a["L0_tok_b_spline"].reshape(1, E),
        "w_base": rows(a["L0_tok_W_base"].T),
        "b_base": a["L0_tok_b_base"].reshape(1, E),
        "w_qkv": rows(a["L0_attn_w_qkv"]),
        "mem_k": np.ascontiguousarray(a["L0_attn_mem_kv"][0].reshape(P, MEM)),
        "mem_v": np.ascontiguousarray(a["L0_attn_mem_kv"][1].reshape(P, MEM).T),
        "w_out": np.ascontiguousarray(a["L0_attn_w_out"]),
        "b_out": a["L0_attn_b_out"].reshape(1, E),
        "g_out": a["L0_attn_g_out"].reshape(1, E),
        "g_pre": np.ascontiguousarray(a["L0_attn_g_pre"].reshape(HALVES, P).T),
        "w_ih": gate_tiles(a["L0_ffn_W_ih"]),
        "w_hh": gate_tiles(a["L0_ffn_W_hh"]),
        "b_ih": gate_row(a["L0_ffn_b_ih"]),
        "b_hh": gate_row(a["L0_ffn_b_hh"]),
        "w_lin": rows(a["L0_ffn_W_lin"].T),
        "b_lin": a["L0_ffn_b_lin"].reshape(1, 2),
        "fw": np.ascontiguousarray(a["L0_ffn_fw_att"].reshape(HALVES, P).T),
        "bw": np.ascontiguousarray(a["L0_ffn_bw_att"].reshape(HALVES, P).T),
    }


def kernel(**inputs):
    import concourse.bacc as bacc
    from concourse.bass_utils import run_bass_kernel_spmd

    arrays = layout(inputs)
    B, T = arrays["x"].shape[0], arrays["x"].shape[2] + arrays["txt"].shape[1]
    nc = bacc.Bacc("TRN2", target_bir_lowering=False, num_devices=1)
    args = [nc.dram_tensor(name, a.shape, mybir.dt.from_np(a.dtype), kind="ExternalInput").ap()
            for name, a in arrays.items()]
    args.append(nc.dram_tensor("out", (B, T, E), F32, kind="ExternalOutput").ap())
    build(nc, *args)
    return run_bass_kernel_spmd(nc, [arrays], core_ids=[0]).results[0]["out"]
```
